# Optimizing a Trainium2 kernel written in Bass

```python
import numpy as np
import jax
import jax.numpy as jnp

def _softmax(x, axis=-1):
    return jax.nn.softmax(x, axis=axis)

def _gelu(x):
    return jax.nn.gelu(x, approximate=True)

def _silu(x):
    return jax.nn.silu(x)

def _sigmoid(x):
    return jax.nn.sigmoid(x)

def _layernorm(x, axis=-1, eps=1e-05):
    m = jnp.mean(x, axis=axis, keepdims=True)
    v = jnp.var(x, axis=axis, keepdims=True)
    return (x - m) / jnp.sqrt(v + eps)

def _scatter_add(tgt, idx, src, axis=0):
    return tgt.at[idx].add(src)

def _segment_sum(src, seg, n):
    return jax.ops.segment_sum(src, seg, n)
kernel_name = 'mk_adj_ffn_d2_adj_r2_ab2a79'

def setup_inputs(seed: int=0):
    np.random.seed(seed)
    _w = jnp.asarray

    def _rec_inputs():
        import jax
        import jax.numpy as jnp
        _gk = jax.random.key(seed)
        x = -0.0005207 + 1.001 * jax.random.normal(jax.random.fold_in(_gk, 1), (4096, 128), jnp.float32)
        _a = jax.random.bernoulli(jax.random.fold_in(_gk, 2), 0.00195312, (4096, 4096))
        _a = jnp.logical_or(_a, jnp.swapaxes(_a, -1, -2))
        _a = jnp.logical_or(_a, jnp.eye(4096, dtype=bool))
        _af = _a.astype(jnp.float32)
        _af = _af * jax.random.uniform(jax.random.fold_in(_gk, 3), (4096, 4096), jnp.float32, 0.05, 1)
        adj = _af
        return (x, adj)
    x, adj = _rec_inputs()

    def _L0_gnn_setup():
        import jax, jax.numpy as jnp
        import numpy as np
        N = 4096
        D = 128
        L = 3

        def _cxin_conv(x, a, eps, W, b):
            ax = a @ x
            h = ax + (1.0 + eps[0]) * ax
            for i in range(L):
                h = jax.nn.relu(h @ W[i].T + b[i])
            return h
        key = jax.random.key(seed)
        ks = jax.random.split(key, 8)
        s = 1.0 / np.sqrt(D)
        return {'x1': jax.random.normal(ks[0], (N, D), jnp.float32), 'x2': jax.random.normal(ks[1], (N, D), jnp.float32), 'G1': jax.random.uniform(ks[2], (N, N), jnp.float32), 'G2': jax.random.uniform(ks[3], (N, N), jnp.float32), 'eps1': jnp.zeros((1,), jnp.float32), 'eps2': jnp.zeros((1,), jnp.float32), 'W1': jax.random.normal(ks[4], (L, D, D), jnp.float32) * s, 'b1': jnp.zeros((L, D), jnp.float32), 'W2': jax.random.normal(ks[5], (L, D, D), jnp.float32) * s, 'b2': jnp.zeros((L, D), jnp.float32), 'Wm': jax.random.normal(ks[6], (D, 2 * D), jnp.float32) * (1.0 / np.sqrt(2 * D)), 'bm': jnp.zeros((D,), jnp.float32)}
    _L0_gnn_all = _L0_gnn_setup()
    _L0_gnn_in = {k: v for k, v in _L0_gnn_all.items() if k in ('x2', 'eps1', 'eps2', 'W1', 'b1', 'W2', 'b2', 'Wm', 'bm')}
    del _L0_gnn_all

    def _L0_ffn_setup():
        import jax, jax.numpy as jnp
        import numpy as np
        B, S, D = (8, 2048, 128)
        H = 4 * D
        CAPACITY = 0.5
        key = jax.random.key(seed)
        ks = jax.random.split(key, 6)
        x = jax.random.normal(ks[0], (B, S, D), dtype=jnp.float32)
        attention_mask = jnp.zeros((B, 1, 1, S), dtype=jnp.float32)
        wr = jax.random.normal(ks[1], (D, 1), dtype=jnp.float32) * 0.02
        br = jnp.zeros((1,), dtype=jnp.float32)
        w1 = jax.random.normal(ks[2], (D, H), dtype=jnp.float32) * 0.02
        b1 = jnp.zeros((H,), dtype=jnp.float32)
        w2 = jax.random.normal(ks[3], (H, D), dtype=jnp.float32) * 0.02
        b2 = jnp.zeros((D,), dtype=jnp.float32)
        return {'x': x, 'attention_mask': attention_mask, 'wr': wr, 'br': br, 'w1': w1, 'b1': b1, 'w2': w2, 'b2': b2}
    _L0_ffn_all = _L0_ffn_setup()
    _L0_ffn_in = {k: v for k, v in _L0_ffn_all.items() if k in ('attention_mask', 'wr', 'br', 'w1', 'b1', 'w2', 'b2')}
    del _L0_ffn_all

    def _L1_gnn_setup():
        import jax, jax.numpy as jnp
        import numpy as np
        N = 4096
        D = 128
        CUTOFF = 1.0
        MU = 1.0
        SIGMA = 0.5

        def sensitivity(r, mu, sigma):
            return jnp.exp(-(1.0 / r - 1.0 / mu) ** 2 / (2.0 * sigma * sigma))
        key = jax.random.key(seed)
        k_z, k_d, k_w = jax.random.split(key, 3)
        z = jax.random.normal(k_z, (N, D), dtype=jnp.float32)
        dist_matrix = jax.random.uniform(k_d, (N, N), dtype=jnp.float32) * 2.0 + 0.05
        W = jax.random.normal(k_w, (D, D), dtype=jnp.float32)
        B = jnp.zeros((D,), dtype=jnp.float32)
        return {'z': z, 'dist_matrix': dist_matrix, 'W': W, 'B': B}
    _L1_gnn_all = _L1_gnn_setup()
    _L1_gnn_in = {k: v for k, v in _L1_gnn_all.items() if k in ('W', 'B')}
    del _L1_gnn_all

    def _L1_ffn_setup():
        import jax, jax.numpy as jnp
        import numpy as np
        B, S, D, H, E, K = (8, 4096, 128, 512, 8, 2)
        key = jax.random.key(seed)
        ks = jax.random.split(key, 7)
        s_in = 1.0 / np.sqrt(D)
        s_hid = 1.0 / np.sqrt(H)
        return {'x': jax.random.normal(ks[0], (B, S, D), dtype=jnp.float32), 'Wg': jax.random.uniform(ks[1], (E, D), jnp.float32, -s_in, s_in), 'bg': jax.random.uniform(ks[2], (E,), jnp.float32, -s_in, s_in), 'W1': jax.random.uniform(ks[3], (E, H, D), jnp.float32, -s_in, s_in), 'b1': jax.random.uniform(ks[4], (E, H), jnp.float32, -s_in, s_in), 'W2': jax.random.uniform(ks[5], (E, D, H), jnp.float32, -s_hid, s_hid), 'b2': jax.random.uniform(ks[6], (E, D), jnp.float32, -s_hid, s_hid)}
    _L1_ffn_all = _L1_ffn_setup()
    _L1_ffn_in = {k: v for k, v in _L1_ffn_all.items() if k in ('Wg', 'bg', 'W1', 'b1', 'W2', 'b2')}
    del _L1_ffn_all
    return {'x': x, 'adj': adj, 'L0_gnn_x2': _L0_gnn_in['x2'], 'L0_gnn_eps1': _L0_gnn_in['eps1'], 'L0_gnn_eps2': _L0_gnn_in['eps2'], 'L0_gnn_W1': _L0_gnn_in['W1'], 'L0_gnn_b1': _L0_gnn_in['b1'], 'L0_gnn_W2': _L0_gnn_in['W2'], 'L0_gnn_b2': _L0_gnn_in['b2'], 'L0_gnn_Wm': _L0_gnn_in['Wm'], 'L0_gnn_bm': _L0_gnn_in['bm'], 'L0_ffn_attention_mask': _L0_ffn_in['attention_mask'], 'L0_ffn_wr': _L0_ffn_in['wr'], 'L0_ffn_br': _L0_ffn_in['br'], 'L0_ffn_w1': _L0_ffn_in['w1'], 'L0_ffn_b1': _L0_ffn_in['b1'], 'L0_ffn_w2': _L0_ffn_in['w2'], 'L0_ffn_b2': _L0_ffn_in['b2'], 'L1_gnn_W': _L1_gnn_in['W'], 'L1_gnn_B': _L1_gnn_in['B'], 'L1_ffn_Wg': _L1_ffn_in['Wg'], 'L1_ffn_bg': _L1_ffn_in['bg'], 'L1_ffn_W1': _L1_ffn_in['W1'], 'L1_ffn_b1': _L1_ffn_in['b1'], 'L1_ffn_W2': _L1_ffn_in['W2'], 'L1_ffn_b2': _L1_ffn_in['b2']}

def reference(x, adj, L0_gnn_x2, L0_gnn_eps1, L0_gnn_eps2, L0_gnn_W1, L0_gnn_b1, L0_gnn_W2, L0_gnn_b2, L0_gnn_Wm, L0_gnn_bm, L0_ffn_attention_mask, L0_ffn_wr, L0_ffn_br, L0_ffn_w1, L0_ffn_b1, L0_ffn_w2, L0_ffn_b2, L1_gnn_W, L1_gnn_B, L1_ffn_Wg, L1_ffn_bg, L1_ffn_W1, L1_ffn_b1, L1_ffn_W2, L1_ffn_b2):
    import jax
    import jax.numpy as jnp

    def _L0_gnn_ref(x1, x2, G1, G2, eps1, eps2, W1, b1, W2, b2, Wm, bm):
        import jax, jax.numpy as jnp
        import numpy as np
        N = 4096
        D = 128
        L = 3

        def _cxin_conv(x, a, eps, W, b):
            ax = a @ x
            h = ax + (1.0 + eps[0]) * ax
            for i in range(L):
                h = jax.nn.relu(h @ W[i].T + b[i])
            return h
        out1 = _cxin_conv(x1, G1, eps1, W1, b1)
        out2 = _cxin_conv(x2, G2, eps2, W2, b2)
        merged = jnp.concatenate((out1, out2), axis=1)
        return merged @ Wm.T + bm

    def _L0_ffn_ref(x, attention_mask, wr, br, w1, b1, w2, b2):
        import jax, jax.numpy as jnp
        import numpy as np
        B, S, D = (8, 2048, 128)
        H = 4 * D
        CAPACITY = 0.5
        b, s, d = x.shape
        weights = (jnp.einsum('bsd,do->bso', x, wr) + br)[..., 0]
        k = max(1, int(CAPACITY * s))
        kk = k - 1 if k > 1 else 1
        _, idx = jax.lax.top_k(weights, k)
        sel_idx = idx[:, :kk]
        sel = jnp.take_along_axis(x, sel_idx[:, :, None], axis=1)
        h = jax.nn.gelu(jnp.einsum('bkd,dh->bkh', sel, w1) + b1)
        y = jnp.einsum('bkh,hd->bkd', h, w2) + b2
        w_sel = jnp.take_along_axis(weights, sel_idx, axis=1)
        y = y * w_sel[..., None]
        batch_idx = jnp.arange(b)[:, None]
        processed = jnp.zeros_like(x).at[batch_idx, sel_idx].set(y)
        return processed + x

    def _L1_gnn_ref(z, dist_matrix, W, B):
        import jax, jax.numpy as jnp
        import numpy as np
        N = 4096
        D = 128
        CUTOFF = 1.0
        MU = 1.0
        SIGMA = 0.5

        def sensitivity(r, mu, sigma):
            return jnp.exp(-(1.0 / r - 1.0 / mu) ** 2 / (2.0 * sigma * sigma))
        msg = z @ W + B
        sens = sensitivity(dist_matrix, MU, SIGMA)
        weights = jnp.where(dist_matrix < CUTOFF, sens, 0.0)
        return weights @ msg

    def _L1_ffn_ref(x, Wg, bg, W1, b1, W2, b2):
        import jax, jax.numpy as jnp
        import numpy as np
        B, S, D, H, E, K = (8, 4096, 128, 512, 8, 2)
        gate_scores = jnp.einsum('bsd,ed->bse', x, Wg) + bg
        topk_scores, topk_idx = jax.lax.top_k(gate_scores, K)
        topk_probs = jax.nn.softmax(topk_scores, axis=-1)
        combine = jnp.sum(topk_probs[..., None] * jax.nn.one_hot(topk_idx, E, dtype=x.dtype), axis=-2)
        out = jnp.zeros_like(x)
        for e in range(E):
            h = jax.nn.relu(jnp.einsum('bsd,hd->bsh', x, W1[e]) + b1[e])
            y = jnp.einsum('bsh,dh->bsd', h, W2[e]) + b2[e]
            out = out + combine[..., e:e + 1] * y
        return out
    x = x + _L0_gnn_ref(_layernorm(x, axis=-1), L0_gnn_x2, adj, adj, L0_gnn_eps1, L0_gnn_eps2, L0_gnn_W1, L0_gnn_b1, L0_gnn_W2, L0_gnn_b2, L0_gnn_Wm, L0_gnn_bm)
    x = x + _L0_ffn_ref(_layernorm(x, axis=-1)[None], L0_ffn_attention_mask, L0_ffn_wr, L0_ffn_br, L0_ffn_w1, L0_ffn_b1, L0_ffn_w2, L0_ffn_b2)[0]
    x = x + _L1_gnn_ref(_layernorm(x, axis=-1), adj, L1_gnn_W, L1_gnn_B)
    x = x + _L1_ffn_ref(_layernorm(x, axis=-1)[None], L1_ffn_Wg, L1_ffn_bg, L1_ffn_W1, L1_ffn_b1, L1_ffn_W2, L1_ffn_b2)[0]
    return x

_drawn_inputs = setup_inputs


def setup_inputs(seed=0):
    import zlib

    import numpy as np

    out = dict(_drawn_inputs(seed))
    spreads = {'L0_gnn_b1': (0.0, 0.1),
     'L0_gnn_b2': (0.0, 0.1),
     'L0_gnn_bm': (0.0, 0.1),
     'L0_ffn_b1': (0.0, 0.8),
     'L0_ffn_b2': (0.0, 0.8),
     'L1_gnn_B': (0.0, 0.709)}
    factors = {'L0_ffn_wr': 6.348,
     'L0_ffn_w1': 8.0,
     'L0_ffn_w2': 8.0,
     'L1_ffn_Wg': 8.0,
     'L1_ffn_bg': 8.0,
     'L1_ffn_W1': 8.0,
     'L1_ffn_b1': 22.758,
     'L1_ffn_W2': 8.0,
     'L1_ffn_b2': 64.0}
    for name, (base, spread) in spreads.items():
        noise = np.random.default_rng([zlib.crc32(name.encode()), seed]).standard_normal(out[name].shape)
        drawn = base * np.exp(spread * noise) if base else spread * noise
        out[name] = jnp.asarray(drawn.astype(out[name].dtype))
    for name, factor in factors.items():
        out[name] = (out[name] * factor).astype(out[name].dtype)
    return out
```

```python
import concourse.bass as bass
from concourse import mybir
from contextlib import ExitStack


class Steps:

    def __init__(self, eng, sem, base):
        self.eng, self.sem, self.base, self.k = eng, sem, base, 0

    def do(self, ins):
        ins.then_inc(self.sem, 1)
        self.k += 1

    def wait(self):
        self.eng.wait_ge(self.sem, self.base + self.k)

    def link(self, ins):
        self.do(ins)
        self.wait()


def build_program(nc, adj_tiles, x_in, x2_in, wpack_in, rows_in, moe_w1_in, moe_w2_in, moe_b2_in, out, cols, rows):
    f32, f32r, bf16 = mybir.dt.float32, mybir.dt.float32r, mybir.dt.bfloat16
    i32, u32 = mybir.dt.int32, mybir.dt.uint32
    ALU = mybir.AluOpType
    ACT = mybir.ActivationFunctionType
    AX = mybir.AxisListType.X
    ds = bass.ds

    N, D = x_in.shape
    P = 128
    T = N // P
    CW = 512
    NC = N // CW
    CT = CW // P
    U1 = 2
    NU1 = T // U1
    U2 = 4
    NU2 = T // U2
    E = moe_b2_in.shape[0]
    HB = 4
    KEEP = N // 2 - 1
    EPS = 1e-5
    A1, R1 = 8, 4
    TINY = 1e-18
    assert NU2 == E == 8 and NU1 == 16

    x_v = x_in.rearrange("(t p) d -> p t d", p=P)
    x2_v = x2_in.rearrange("(t p) d -> p t d", p=P)
    out_v = out.rearrange("(c t p) d -> c p t d", t=CT, p=P)

    ctx = ExitStack()
    with ctx:
        def sb(name, shape, dt=f32):
            return ctx.enter_context(nc.sbuf_tensor(name, shape, dt))

        def sem(name):
            return ctx.enter_context(nc.semaphore(name))

        wp = sb("wp", [P, wpack_in.shape[1]])
        rw = sb("rw", [P, rows_in.shape[1]])
        ident = sb("ident", [P, P])
        ones = sb("ones", [P, P])
        before = sb("before", [P, P])
        XU = sb("XU", [P, T, D])
        VM = sb("VM", [P, T, D])
        ms = sb("ms", [P, 2, CW])
        hT = sb("hT", [P, HB, CW])
        z = sb("z", [P, CT, D])
        zT = sb("zT", [P, CW])
        zhi = sb("zhi", [P, CW], f32r)
        zlo = sb("zlo", [P, CW], f32r)
        x3 = sb("x3", [P, CT, D])
        scaled = sb("scaled", [P, CT, D])
        acc = sb("acc", [P, CT, D])
        bn6 = sb("bn6", [P, T, 6])
        mv = sb("mv", [P, T, 2])
        rs_v = sb("rs_v", [P, T])
        rs_y = sb("rs_y", [P, T])
        rs_t = sb("rs_t", [P, T])
        scale12 = sb("scale12", [P, 2])
        cb = sb("cb", [P, 2])
        wtok = sb("wtok", [P, T])
        key = sb("key", [P, T], i32)
        keyt = sb("keyt", [P, T], i32)
        khi = sb("khi", [P, T])
        klo = sb("klo", [P, T])
        steps15 = sb("steps15", [P, 15])
        steps15i = sb("steps15i", [P, 15], i32)
        thr = sb("thr", [P, 15])
        cmp = sb("cmp", [P, 15, T])
        cnt = sb("cnt", [P, 15])
        digit = sb("digit", [P, 1])
        Thi = sb("Thi", [P, 1])
        Tlo = sb("Tlo", [P, 1])
        kleft = sb("kleft", [P, 1])
        above = sb("above", [P, T])
        eqc = sb("eqc", [P, T + 1])
        tots = sb("tots", [P, T])
        rank = sb("rank", [P, T])
        sel = sb("sel", [P, T])
        gate = sb("gate", [P, CT, E])
        top8 = sb("top8", [P, CT, E])
        top8i = sb("top8i", [P, CT, E], u32)
        topf = sb("topf", [P, CT, E])
        iota8 = sb("iota8", [P, CT, E])
        iota8i = sb("iota8i", [P, E], i32)
        pd = sb("pd", [P, CT])
        pe2 = sb("pe2", [P, CT])
        ps1 = sb("ps1", [P, CT])
        prob = sb("prob", [P, 2, CT])
        hot = sb("hot", [P, CT, E])
        comb = sb("comb", [P, CT, E])
        gap = sb("gap", [P, 1])
        cTs = sb("cTs", [E, CW])
        mb2 = sb("mb2", [E, D])

        first = ExitStack()
        raw = [first.enter_context(nc.sbuf_tensor(f"raw{s}", [P, U1 * CW], f32)) for s in range(A1)]
        ahi = [first.enter_context(nc.sbuf_tensor(f"ahi{s}", [P, U1 * CW], f32r)) for s in range(R1)]
        alo = [first.enter_context(nc.sbuf_tensor(f"alo{s}", [P, U1 * CW], f32r)) for s in range(R1)]
        xhi = [first.enter_context(nc.sbuf_tensor(f"xhi{b}", [P, T, D], f32r)) for b in range(2)]
        xlo = [first.enter_context(nc.sbuf_tensor(f"xlo{b}", [P, T, D], f32r)) for b in range(2)]
        first.close()
        wt = [sb(f"wt{u}", [P, U2 * CW]) for u in range(NU2)]
        w1hi = sb("w1hi", [P, E, HB * P], f32r)
        w1lo = sb("w1lo", [P, E, HB * P], f32r)
        w1raw = sb("w1raw", [P, E, HB * P])
        w2 = sb("w2", [P, E, HB, D])

        bank = [ctx.enter_context(nc.psum_tensor(f"bank{i}", [P, 512], f32)) for i in range(8)]

        def W(name):
            a, b = cols[name]
            return wp[:, a:b]

        def R(name):
            a, b = rows[name]
            return rw[:, a:b]

        gnnw = [[wp[:, cols[f"gnn{b}"][0] + D * i:cols[f"gnn{b}"][0] + D * (i + 1)] for i in range(3)] for b in range(2)]
        mergew = [wp[:, cols["merge"][0] + D * b:cols["merge"][0] + D * (b + 1)] for b in range(2)]

        x_in_s, x2_in_s, wp_in, rw_in = sem("x_loaded"), sem("x2_loaded"), sem("wp_loaded"), sem("rows_loaded")
        adj_in = [sem(f"adj_in{s}") for s in range(A1)]
        w_in = [sem(f"wt_in{u}") for u in range(NU2)]
        moe1_in, moe2_in, moeb_in = sem("moe_w1_in"), sem("moe_w2_in"), sem("moe_b2_in")
        stored = sem("stored")
        consts = sem("consts")
        consts_v = sem("consts_v")
        x2hi_r, x2lo_r, xn_r, x1hi_r, x1lo_r = sem("x2hi"), sem("x2lo"), sem("xn"), sem("x1hi"), sem("x1lo")
        hi_ready, lo_ready, unit_done = sem("hi_ready"), sem("lo_ready"), sem("unit_done")
        ax0_done, ax_evac, lay_done, m_ready = sem("ax0_done"), sem("ax_evac"), sem("lay_done"), sem("m_ready")
        merge_done, z1_ready, zT_done, zT_ready = sem("merge_done"), sem("z1_ready"), sem("zT_done"), sem("zT_ready")
        up_done, h_ready, down_done, v_done = sem("up_done"), sem("h_ready"), sem("down_done"), sem("v_done")
        cnt_ready, cnt_done = sem("cnt_ready"), sem("cnt_done")
        z2_ready, z2T_done, z2T_ready, msg_done, msg_ready = sem("z2_ready"), sem("z2T_done"), sem("z2T_ready"), sem("msg_done"), sem("msg_ready")
        msk_ready, ln_done, rec_done, q_ready, wt_ready, wt_used = sem("msk_ready"), sem("ln_done"), sem("rec_done"), sem("q_ready"), sem("wt_ready"), sem("wt_used")
        w1_ready = sem("w1_ready")
        g_evac, t1_done, z3_ready, t2_done, zhi_ready, zlo_ready = sem("g_evac"), sem("t1_done"), sem("z3_ready"), sem("t2_done"), sem("zhi_ready"), sem("zlo_ready")
        gate_done, diff_ready, exp_ready, comb_ready, cT_done, cT_ready, b2_done = sem("gate_done"), sem("diff_ready"), sem("exp_ready"), sem("comb_ready"), sem("cT_done"), sem("cT_ready"), sem("b2_done")
        up2_done, h2_ready, down2_done, y_used, acc_done = sem("up2_done"), sem("h2_ready"), sem("down2_done"), sem("y_used"), sem("acc_done")
        dve_s, pool_s = sem("dve_steps"), sem("pool_steps")

        block = ctx.enter_context(nc.Block())

        ALL1 = NC * NU1

        def has(chunk, c):
            return not isinstance(c, int) or 0 <= chunk < NC

        def expert_at(c, u):
            o, e = (c - 2, E - 2 + u) if u < 2 else (c - 1, u - 2)
            return (o, e) if has(o, c) else None

        @block.sync
        def _(sp):
            sp.dma_start(VM[:, :, :], x2_v).then_inc(x2_in_s, 16)
            sp.dma_start(XU[:, :, :], x_v).then_inc(x_in_s, 16)
            sp.dma_start(rw[:, :], rows_in[0, :].partition_broadcast(P)).then_inc(rw_in, 16)

            def load1(c, p, off):
                if not isinstance(c, int) or c * NU1 + p >= A1:
                    sp.wait_ge(lo_ready, c * NU1 + p - (A1 - 1))
                sp.dma_start(raw[p % A1][:, :], adj_tiles[off, :, :]).then_inc(adj_in[p % A1], 16)

            for p in range(NU1):
                load1(0, p, p)
                if p == 3:
                    sp.dma_start(wp[:, :], wpack_in[:, :]).then_inc(wp_in, 16)
            with sp.Fori(1, NC) as c:
                for p in range(NU1):
                    off = sp.snap(c * NU1 + p)
                    sp.wait_ge(lo_ready, c * NU1 + p - (A1 - 1))
                    sp.dma_start(raw[p % A1][:, :].rearrange("p (a f) -> p a f", a=1),
                                 adj_tiles[ds(off, 1), :, :].rearrange("a p f -> p a f")).then_inc(adj_in[p % A1], 16)

            sp.wait_ge(unit_done, ALL1)

            def load2(cc, u):
                src = adj_tiles[ds(cc * NU1 + 2 * u, 2), :, :] if not isinstance(cc, int) else adj_tiles[cc * NU1 + 2 * u:cc * NU1 + 2 * u + 2, :, :]
                return sp.dma_start(wt[u][:, :].rearrange("p (a f) -> p a f", a=2), src.rearrange("a p f -> p a f")).then_inc(w_in[u], 16)

            for u in range(NU2):
                load2(0, u)
                if u == 3:
                    sp.dma_start(w1raw[:, :, :], moe_w1_in[:, :, :]).then_inc(moe1_in, 16)
            sp.dma_start(w2[:, :, :, :], moe_w2_in[:, :, :, :]).then_inc(moe2_in, 16)
            sp.dma_start(mb2[:, :], moe_b2_in[:, :]).then_inc(moeb_in, 16)

            def store(o, ro):
                sp.wait_ge(acc_done, o + 1)
                dst = out_v[o, :, :, :] if isinstance(o, int) else out_v[ds(ro, 1), :, :, :].rearrange("a p t d -> p (a t) d")
                sp.dma_start(dst, acc[:, :, :]).then_inc(stored, 16)

            def iteration(c):
                for u in range(NU2):
                    if not isinstance(c, int):
                        off = sp.snap(c * NU1 + NU1 + 2 * u)
                        sp.wait_ge(wt_used, c * NU2 + u + 1)
                        sp.dma_start(wt[u][:, :].rearrange("p (a f) -> p a f", a=2),
                                     adj_tiles[ds(off, 2), :, :].rearrange("a p f -> p a f")).then_inc(w_in[u], 16)
                    elif c + 1 < NC:
                        sp.wait_ge(wt_used, c * NU2 + u + 1)
                        load2(c + 1, u)
                    if u == 2 and has(c - 2, c):
                        store(c - 2, None if isinstance(c, int) else sp.snap(c - 2))

            iteration(0)
            iteration(1)
            with sp.Fori(2, NC - 1) as c:
                iteration(c)
            for c in range(NC - 1, NC + 2):
                iteration(c)
            sp.wait_ge(stored, 16 * NC)

        @block.gpsimd
        def _(pool):
            own = Steps(pool, pool_s, 0)
            own.do(pool.memset(ident[:, :], 0.0))
            pool.memset(ones[:, :], 1.0).then_inc(consts, 1)
            own.do(pool.memset(before[:, :], 1.0))
            own.do(pool.iota(steps15i[:, :], pattern=[[1, 15]], base=1, channel_multiplier=0))
            own.do(pool.iota(iota8i[:, :], pattern=[[1, E]], base=0, channel_multiplier=0))
            own.wait()
            pool.affine_select(out=ident[:, :], in_=ident[:, :], compare_op=ALU.not_equal, fill=1.0, base=0,
                               pattern=[[-1, P]], channel_multiplier=1).then_inc(consts, 1)
            pool.affine_select(out=before[:, :], in_=before[:, :], compare_op=ALU.is_ge, fill=0.0, base=-1,
                               pattern=[[1, P]], channel_multiplier=-1).then_inc(consts, 1)
            pool.tensor_copy(steps15[:, :], steps15i[:, :]).then_inc(consts, 1)
            for t in range(CT):
                pool.tensor_copy(iota8[:, t, :], iota8i[:, :]).then_inc(consts, 1)
            for g in range(NC):
                s = slice(g * CT, (g + 1) * CT)
                pool.wait_ge(x2hi_r, g + 1)
                pool.tensor_tensor(xlo[1][:, s, :], VM[:, s, :], xhi[1][:, s, :].bitcast(f32), ALU.subtract).then_inc(x2lo_r, 1)
            pool.wait_ge(moe1_in, 16)
            own.link(pool.tensor_copy(w1hi[:, :, :], w1raw[:, :, :]))
            pool.tensor_tensor(w1lo[:, :, :], w1raw[:, :, :], w1hi[:, :, :].bitcast(f32), ALU.subtract).then_inc(w1_ready, 1)

        @block.scalar
        def _(act):
            act.wait_ge(x2_in_s, 16)
            for g in range(NC):
                s = slice(g * CT, (g + 1) * CT)
                act.activation(xhi[1][:, s, :], VM[:, s, :], ACT.Copy).then_inc(x2hi_r, 1)

            def hi(c, p):
                act.wait_ge(adj_in[p % A1], 16 * (2 * c + p // A1 + 1))
                if not isinstance(c, int) or c * NU1 + p >= R1:
                    act.wait_ge(unit_done, c * NU1 + p - (R1 - 1))
                act.activation(ahi[p % R1][:, :], raw[p % A1][:, :], ACT.Copy).then_inc(hi_ready, 1)

            def first_pass(c, main, post):
                for p in range(NU1):
                    if c is 0 and p % 2 == 0:
                        g = p // 2
                        act.wait_ge(xn_r, CT * (g + 1))
                        act.activation(xhi[0][:, g * CT:(g + 1) * CT, :], hT[:, g % 4, :], ACT.Copy).then_inc(x1hi_r, 1)
                    if main and p != 3:
                        hi(c, p)
                    if post and p == 2:
                        act.wait_ge(ax0_done, c)
                        act.activation(ms[:, 0, :], bank[0][:, :], ACT.Copy, scale=scale12[:, 0:1]).then_inc(ax_evac, 1)
                        act.wait_ge(unit_done, c * NU1)
                        act.activation(ms[:, 1, :], bank[1][:, :], ACT.Copy, scale=scale12[:, 1:2]).then_inc(ax_evac, 1)
                    if main and p == 3:
                        hi(c, p)
                    if post and p in (3, 5, 7):
                        i = (p - 3) // 2
                        act.wait_ge(lay_done, 3 * c - 3 + i + 1)
                        for b in range(2):
                            a = cols[f"gnnb{b}"][0] + i
                            act.activation(ms[:, b, :], bank[2 + b][:, :], ACT.Relu, bias=wp[:, a:a + 1]).then_inc(m_ready, 1)
                    if post and p == 12:
                        act.wait_ge(zT_done, c)
                        act.activation(zT[:, :], bank[5][:, :], ACT.Copy).then_inc(zT_ready, 1)
                    if post and p == 14:
                        for k in range(HB):
                            a = cols["ffn_b1"][0] + k
                            act.wait_ge(up_done, HB * c - HB + k + 1)
                            act.activation(hT[:, k, :], bank[(2, 3, 6, 7)[k]][:, :], ACT.Gelu_apprx_tanh,
                                           bias=wp[:, a:a + 1]).then_inc(h_ready, 1)

            first_pass(0, True, False)
            with act.Fori(1, NC) as c:
                first_pass(c, True, True)
            first_pass(NC, False, True)

            def ln(cc, u):
                act.wait_ge(msk_ready, cc * NU2 + u + 1)
                act.activation(wt[u][:, :], wt[u][:, :], ACT.Ln, bias=cb[:, 0:1]).then_inc(ln_done, 1)

            def rec(cc, u):
                act.wait_ge(ln_done, cc * NU2 + u + 1)
                act.activation(wt[u][:, :], wt[u][:, :], ACT.Exp, scale=-1.0).then_inc(rec_done, 1)

            def sens(cc, u):
                act.wait_ge(q_ready, cc * NU2 + u + 1)
                act.activation(wt[u][:, :], wt[u][:, :], ACT.Exp, scale=-2.0, bias=cb[:, 1:2]).then_inc(wt_ready, 1)

            for u in range(4):
                ln(0, u)
            for u in range(4):
                rec(0, u)
            for u in range(4):
                sens(0, u)

            with act.Fori(0, NC) as g:
                act.wait_ge(z2T_done, g + 1)
                act.activation(zT[:, :], bank[5][:, :], ACT.Copy).then_inc(z2T_ready, 1)

            def iteration(c):
                for u in range(NU2):
                    if u == 0 and has(c - 1, c):
                        act.wait_ge(wt_used, c * NU2)
                        act.activation(ms[:, 0, :], bank[0][:, :], ACT.Copy).then_inc(g_evac, 1)
                    if (oe := expert_at(c, u)):
                        o, e = oe
                        for k in range(HB):
                            a = cols["moe_b1"][0] + HB * e + k
                            act.wait_ge(up2_done, o * (E * HB) + HB * e + k + 1)
                            act.activation(hT[:, k, :], bank[1 + k][:, :], ACT.Relu, bias=wp[:, a:a + 1]).then_inc(h2_ready, 1)
                    if u == 1 and has(c - 1, c):
                        act.wait_ge(t2_done, c)
                        act.activation(zT[:, :], bank[7][:, :], ACT.Copy).then_inc(zhi_ready, 1)
                        act.activation(zhi[:, :], bank[7][:, :], ACT.Copy).then_inc(zhi_ready, 1)
                    if u == 2 and has(c - 1, c):
                        act.wait_ge(diff_ready, c)
                        act.activation(pe2[:, :], pd[:, :], ACT.Exp).then_inc(exp_ready, 1)
                    if u == 3 and has(c - 1, c):
                        act.wait_ge(cT_done, c)
                        act.activation(cTs[:, :], bank[7][0:E, :], ACT.Copy).then_inc(cT_ready, 1)
                    half, k = u // 4, u % 4
                    if has(c + half, c):
                        cc, b = c + half, 4 * (1 - half)
                        for fn, j in (((ln, 0), (ln, 1), (ln, 2)), ((ln, 3), (rec, 0), (rec, 1)),
                                      ((rec, 2), (rec, 3), (sens, 0)), ((sens, 1), (sens, 2), (sens, 3)))[k]:
                            fn(cc, b + j)

            iteration(0)
            iteration(1)
            with act.Fori(2, NC - 1) as c:
                iteration(c)
            for c in range(NC - 1, NC + 2):
                iteration(c)

        @block.vector
        def _(dve):
            own = Steps(dve, dve_s, 0)

            def rsqrt(own, var, n):
                v, y, t = rs_v[:, 0:n], rs_y[:, 0:n], rs_t[:, 0:n]
                own.link(dve.tensor_scalar(v, var, EPS, None, ALU.add))
                own.link(dve.tensor_scalar(t.bitcast(i32), v.bitcast(i32), 1, None, ALU.logical_shift_right))
                own.link(dve.tensor_scalar(y.bitcast(i32), t.bitcast(i32), -1.0, 1597463007.0, ALU.mult, ALU.add))
                for _ in range(4):
                    own.link(dve.scalar_tensor_tensor(out=t, in0=y, scalar=0.5, in1=y, op0=ALU.mult, op1=ALU.mult))
                    own.link(dve.tensor_tensor(t, t, v, ALU.mult))
                    own.link(dve.scalar_tensor_tensor(out=y, in0=t, scalar=1.5, in1=y, op0=ALU.subtract, op1=ALU.mult))

            def moments(own, n):
                b, m, v = bn6[:, 0:n, :], mv[:, 0:n, 0], mv[:, 0:n, 1]
                own.do(dve.tensor_tensor(m, b[:, :, 1], b[:, :, 4], ALU.add))
                own.do(dve.tensor_tensor(rs_t[:, 0:n], b[:, :, 2], b[:, :, 5], ALU.add))
                own.link(dve.tensor_tensor(rs_y[:, 0:n], b[:, :, 1], b[:, :, 4], ALU.subtract))
                own.do(dve.tensor_scalar(m, m, 0.5, None, ALU.mult))
                own.link(dve.scalar_tensor_tensor(out=rs_y[:, 0:n], in0=rs_y[:, 0:n], scalar=0.25, in1=rs_y[:, 0:n],
                                                  op0=ALU.mult, op1=ALU.mult))
                own.link(dve.scalar_tensor_tensor(out=v, in0=rs_t[:, 0:n], scalar=1.0 / D, in1=rs_y[:, 0:n],
                                                  op0=ALU.mult, op1=ALU.add))

            def stats(own, src, n):
                for k in range(n):
                    own.do(dve.bn_stats(bn6[:, k, :], src(k)))
                own.wait()
                moments(own, n)

            own.do(dve.memset(cb[:, 0:1], TINY))
            own.do(dve.memset(cb[:, 1:2], -2.0))
            dve.wait_ge(x_in_s, 16)
            stats(own, lambda k: XU[:, k, :], T)
            rsqrt(own, mv[:, :, 1], T)
            dve.wait_ge(rw_in, 16)
            dve.tensor_scalar(scale12[:, :], R("eps"), 1.0, 1.0, ALU.add, ALU.add).then_inc(consts_v, 1)

            def lo(c, p):
                dve.wait_ge(hi_ready, c * NU1 + p + 1)
                dve.tensor_tensor(alo[p % R1][:, :], raw[p % A1][:, :], ahi[p % R1][:, :].bitcast(f32), ALU.subtract).then_inc(lo_ready, 1)

            def norm_x(g):
                if g >= 4:
                    dve.wait_ge(x1lo_r, g - 3)
                for k in range(CT):
                    t = g * CT + k
                    dve.tensor_scalar(hT[:, g % 4, k * D:(k + 1) * D], XU[:, t, :], mv[:, t, 0:1], rs_y[:, t:t + 1],
                                      ALU.subtract, ALU.mult).then_inc(xn_r, 1)
                dve.wait_ge(x1hi_r, g + 1)
                dve.tensor_tensor(xlo[0][:, g * CT:(g + 1) * CT, :], hT[:, g % 4, :],
                                  xhi[0][:, g * CT:(g + 1) * CT, :].bitcast(f32), ALU.subtract).then_inc(x1lo_r, 1)

            def tiles(c, back):
                return slice((c - back) * CT, (c - back + 1) * CT) if isinstance(c, int) else ds((c - back) * CT, CT)

            def first_pass(c, main, post, own):
                for p in range(NU1):
                    if c is 0 and p % 2 == 0:
                        norm_x(p // 2)
                    if main:
                        lo(c, p)
                    if post and p == 10:
                        u = XU[:, tiles(c, 1), :]
                        dve.wait_ge(merge_done, c)
                        own.link(dve.tensor_tensor(x3[:, :, :], bank[4][:, :].rearrange("p (t d) -> p t d", t=CT), u, ALU.add))
                        stats(own, lambda k: x3[:, k, :], CT)
                        rsqrt(own, mv[:, 0:CT, 1], CT)
                        for k in range(CT):
                            dve.tensor_scalar(z[:, k, :], x3[:, k, :], mv[:, k, 0:1], rs_y[:, k:k + 1], ALU.subtract, ALU.mult).then_inc(z1_ready, 1)
                        dve.wait_ge(z1_ready, CT * c)
                        own.link(dve.tensor_tensor(u, x3[:, :, :], z[:, :, :], ALU.add))
                    if post and p == 15:
                        y = VM[:, tiles(c, 1), :]
                        wv = wtok[:, tiles(c, 1)]
                        dve.wait_ge(down_done, c)
                        own.do(dve.tensor_tensor(wv, bank[4][:, 0:CT], R("br").to_broadcast([P, CT]), ALU.add))
                        own.link(dve.tensor_tensor(y, bank[5][:, :].rearrange("p (t d) -> p t d", t=CT),
                                                   R("ffn_b2").unsqueeze(1).to_broadcast([P, CT, D]), ALU.add))
                        dve.tensor_tensor(y, y, wv.unsqueeze(2).to_broadcast([P, CT, D]), ALU.mult).then_inc(v_done, 1)

            PER1 = 1 + CT + 6 + 15 + 1 + 2
            first_pass(0, True, False, own)
            dve.tensor_tensor(XU[:, :, :], XU[:, :, :], R("bm").unsqueeze(1).to_broadcast([P, T, D]), ALU.add).then_inc(v_done, 1)
            dve.wait_ge(v_done, 1)
            k0 = own.k
            with dve.Fori(1, NC) as c:
                it = Steps(dve, dve_s, (c - 1) * PER1 + k0)
                first_pass(c, True, True, it)
                assert it.k == PER1, it.k
            own.k = k0 + (NC - 1) * PER1

            def mask(cc, u):
                dve.wait_ge(w_in[u], 16 * (cc + 1))
                dve.scalar_tensor_tensor(out=wt[u][:, :], in0=wt[u][:, :], scalar=1.0, in1=wt[u][:, :],
                                         op0=ALU.is_lt, op1=ALU.mult).then_inc(msk_ready, 1)

            def square(cc, u):
                dve.wait_ge(rec_done, cc * NU2 + u + 1)
                dve.scalar_tensor_tensor(out=wt[u][:, :], in0=wt[u][:, :], scalar=2.0, in1=wt[u][:, :],
                                         op0=ALU.subtract, op1=ALU.mult).then_inc(q_ready, 1)

            first_pass(NC, False, True, own)
            for u in range(6):
                mask(0, u)

            dve.wait_ge(consts, 4 + CT)
            dve.wait_ge(v_done, NC + 1)
            own.link(dve.tensor_scalar(keyt[:, :], wtok[:, :].bitcast(i32), 31, -2147483648, ALU.arith_shift_right, ALU.bitwise_or))
            own.link(dve.tensor_tensor(key[:, :], wtok[:, :].bitcast(i32), keyt[:, :], ALU.bitwise_xor))
            own.link(dve.tensor_scalar(keyt[:, :], key[:, :], 16, None, ALU.logical_shift_right))
            own.link(dve.tensor_copy(khi[:, :], keyt[:, :]))
            own.link(dve.tensor_scalar(key[:, :], key[:, :], 65535, None, ALU.bitwise_and))
            own.link(dve.tensor_copy(klo[:, :], key[:, :]))
            own.do(dve.memset(Thi[:, :], 0.0))
            own.do(dve.memset(Tlo[:, :], 1.0))
            own.link(dve.memset(kleft[:, :], float(KEEP)))
            asked = [0]

            def count(ins):
                ins.then_inc(cnt_ready, 1)
                asked[0] += 1
                dve.wait_ge(cnt_done, asked[0])

            def search(vals, t_ap):
                for shift in (12, 8, 4, 0):
                    own.link(dve.tensor_scalar(thr[:, :], steps15[:, :], float(1 << shift), t_ap, ALU.mult, ALU.add))
                    own.link(dve.tensor_tensor(cmp[:, :, :], vals.unsqueeze(1).to_broadcast([P, 15, T]),
                                               thr[:, :].unsqueeze(2).to_broadcast([P, 15, T]), ALU.is_ge))
                    count(dve.tensor_reduce(out=cnt[:, :], in_=cmp[:, :, :], op=ALU.add, axis=AX))
                    own.link(dve.tensor_scalar(thr[:, :], bank[6][:, 0:15], kleft[:, :], None, ALU.is_ge))
                    own.link(dve.tensor_reduce(out=digit[:, :], in_=thr[:, :], op=ALU.add, axis=AX))
                    own.link(dve.scalar_tensor_tensor(out=t_ap, in0=digit[:, :], scalar=float(1 << shift), in1=t_ap,
                                                      op0=ALU.mult, op1=ALU.add))

            search(khi[:, :], Thi[:, :])
            own.link(dve.tensor_scalar(above[:, :], khi[:, :], Thi[:, :], None, ALU.is_gt))
            count(dve.tensor_reduce(out=cnt[:, 0:1], in_=above[:, :], op=ALU.add, axis=AX))
            own.do(dve.tensor_scalar(kleft[:, :], bank[6][:, 0:1], -1.0, float(KEEP), ALU.mult, ALU.add))
            own.link(dve.tensor_scalar(klo[:, :], klo[:, :], 1.0, None, ALU.add))
            own.link(dve.scalar_tensor_tensor(out=klo[:, :], in0=khi[:, :], scalar=Thi[:, :], in1=klo[:, :],
                                              op0=ALU.is_equal, op1=ALU.mult))
            search(klo[:, :], Tlo[:, :])
            own.do(dve.scalar_tensor_tensor(out=above[:, :], in0=klo[:, :], scalar=Tlo[:, :], in1=above[:, :],
                                            op0=ALU.is_gt, op1=ALU.add))
            own.link(dve.tensor_scalar(eqc[:, 0:T], klo[:, :], Tlo[:, :], None, ALU.is_equal))
            count(dve.tensor_reduce(out=eqc[:, T:T + 1], in_=above[:, :], op=ALU.add, axis=AX))
            own.do(dve.tensor_scalar(kleft[:, :], bank[6][:, T:T + 1], -1.0, float(KEEP), ALU.mult, ALU.add))
            own.link(dve.tensor_copy(rank[:, :], bank[6][:, 0:T]))
            own.link(dve.tensor_tensor_scan(tots[:, :], ones[:, 0:T], rank[:, :], 0.0, ALU.mult, ALU.add))
            own.link(dve.tensor_tensor(tots[:, :], tots[:, :], rank[:, :], ALU.subtract))
            own.link(dve.tensor_tensor(rank[:, :], bank[6][:, 64:64 + T], tots[:, :], ALU.add))
            own.link(dve.scalar_tensor_tensor(out=sel[:, :], in0=rank[:, :], scalar=kleft[:, :], in1=eqc[:, 0:T],
                                              op0=ALU.is_lt, op1=ALU.mult))
            own.link(dve.tensor_tensor(sel[:, :], sel[:, :], above[:, :], ALU.add))

            PER2 = CT
            k0 = own.k
            with dve.Fori(0, NC) as g:
                it = Steps(dve, dve_s, g * PER2 + k0)
                for k in range(CT):
                    t = g * CT + k
                    it.do(dve.scalar_tensor_tensor(out=XU[:, ds(t, 1), :], in0=VM[:, ds(t, 1), :], scalar=sel[:, ds(t, 1)],
                                                   in1=XU[:, ds(t, 1), :], op0=ALU.mult, op1=ALU.add))
            own.k = k0 + NC * PER2
            own.wait()
            k0 = own.k
            with dve.Fori(0, NC) as g:
                it = Steps(dve, dve_s, g * CT + k0)
                for k in range(CT):
                    it.do(dve.bn_stats(bn6[:, ds(g * CT + k, 1), :], XU[:, ds(g * CT + k, 1), :]))
            own.k = k0 + T
            own.wait()
            moments(own, T)
            rsqrt(own, mv[:, :, 1], T)
            for u in range(4):
                square(0, u)
            with dve.Fori(0, NC) as g:
                for k in range(CT):
                    t = g * CT + k
                    dve.tensor_scalar(z[:, k:k + 1, :], XU[:, ds(t, 1), :], mv[:, ds(t, 1), 0], rs_y[:, ds(t, 1)],
                                      ALU.subtract, ALU.mult).then_inc(z2_ready, 1)
                dve.wait_ge(msg_done, g + 1)
                dve.tensor_tensor(VM[:, ds(g * CT, CT), :], bank[4][:, :].rearrange("p (t d) -> p t d", t=CT),
                                  R("B").unsqueeze(1).to_broadcast([P, CT, D]), ALU.add).then_inc(msg_ready, 1)

            def chunk_norm(c, own):
                dve.wait_ge(t1_done, c)
                own.link(dve.tensor_tensor(x3[:, :, :], bank[6][:, :].rearrange("p (t d) -> p t d", t=CT),
                                           XU[:, tiles(c, 1), :], ALU.add))
                stats(own, lambda k: x3[:, k, :], CT)
                rsqrt(own, mv[:, 0:CT, 1], CT)
                for k in range(CT):
                    dve.tensor_scalar(z[:, k, :], x3[:, k, :], mv[:, k, 0:1], rs_y[:, k:k + 1],
                                      ALU.subtract, ALU.mult).then_inc(z3_ready, 1)

            def choose(c, own):
                dve.wait_ge(gate_done, c)
                own.link(dve.tensor_tensor(gate[:, :, :], bank[7][:, 0:CT * E].rearrange("p (t e) -> p t e", t=CT),
                                           R("bg").unsqueeze(1).to_broadcast([P, CT, E]), ALU.add))
                dve.memset(gap[:, :], 0.0)
                for t in range(CT):
                    own.do(dve.max(top8[:, t, :], gate[:, t, :]))
                own.wait()
                dve.tensor_tensor(pd[:, :], top8[:, :, 1], top8[:, :, 0], ALU.subtract).then_inc(diff_ready, 1)
                for t in range(CT):
                    own.do(dve.max_index(top8i[:, t, :], top8[:, t, :], gate[:, t, :]))
                own.wait()
                own.link(dve.tensor_copy(topf[:, :, :], top8i[:, :, :]))

            def combine_weights(c, own):
                dve.wait_ge(exp_ready, c)
                own.link(dve.tensor_scalar(ps1[:, :], pe2[:, :], 1.0, None, ALU.add))
                own.link(dve.reciprocal(prob[:, 0, :], ps1[:, :]))
                own.link(dve.tensor_tensor(prob[:, 1, :], pe2[:, :], prob[:, 0, :], ALU.mult))
                own.do(dve.tensor_tensor(hot[:, :, :], iota8[:, :, :], topf[:, :, 0:1].to_broadcast([P, CT, E]), ALU.is_equal))
                own.link(dve.tensor_tensor(comb[:, :, :], iota8[:, :, :], topf[:, :, 1:2].to_broadcast([P, CT, E]), ALU.is_equal))
                own.do(dve.tensor_tensor(hot[:, :, :], hot[:, :, :], prob[:, 0, :].unsqueeze(2).to_broadcast([P, CT, E]), ALU.mult))
                own.link(dve.tensor_tensor(comb[:, :, :], comb[:, :, :], prob[:, 1, :].unsqueeze(2).to_broadcast([P, CT, E]), ALU.mult))
                dve.tensor_tensor(comb[:, :, :], comb[:, :, :], hot[:, :, :], ALU.add).then_inc(comb_ready, 1)
                dve.wait_ge(comb_ready, c)

            def combine(c, o, e, own):
                dve.wait_ge(down2_done, o * E + e + 1)
                dve.tensor_tensor(scaled[:, :, :], bank[5][:, :].rearrange("p (t d) -> p t d", t=CT),
                                  comb[:, :, e:e + 1].to_broadcast([P, CT, D]), ALU.mult).then_inc(y_used, 1)
                dve.wait_ge(y_used, o * E + e + 1)
                if e == 0:
                    if not isinstance(o, int) or o >= 1:
                        dve.wait_ge(stored, 16 * o)
                    own.link(dve.tensor_tensor(acc[:, :, :], x3[:, :, :], scaled[:, :, :], ALU.add))
                elif e < E - 1:
                    own.link(dve.tensor_tensor(acc[:, :, :], acc[:, :, :], scaled[:, :, :], ALU.add))
                else:
                    dve.tensor_tensor(acc[:, :, :], acc[:, :, :], scaled[:, :, :], ALU.add).then_inc(acc_done, 1)

            def iteration(c, own):
                for u in range(NU2):
                    new = has(c - 1, c)
                    if u == 0 and new:
                        chunk_norm(c, own)
                    if u == 1 and new:
                        dve.wait_ge(zhi_ready, 2 * c)
                        dve.tensor_tensor(zlo[:, :], zT[:, :], zhi[:, :].bitcast(f32), ALU.subtract).then_inc(zlo_ready, 1)
                    if u == 2 and new:
                        combine_weights(c, own)
                    if u == 5 and new:
                        dve.wait_ge(b2_done, c)
                        own.link(dve.tensor_tensor(acc[:, :, :], acc[:, :, :], bank[6][:, :].rearrange("p (t d) -> p t d", t=CT), ALU.add))
                    if (oe := expert_at(c, u)):
                        combine(c, *oe, own)
                    if u == 1 and new:
                        choose(c, own)
                    half, k = u // 4, u % 4
                    if has(c + half, c):
                        cc, b = c + half, 4 * (1 - half)
                        if k < 2:
                            mask(cc, b + 2 + k)
                        else:
                            square(cc, b + 2 * k - 4)
                            square(cc, b + 2 * k - 3)
                    if k == 3 and has(c + 1, c):
                        mask(c + 1, 4 * half)
                        mask(c + 1, 4 * half + 1)

            iteration(0, own)
            iteration(1, own)
            k0 = own.k
            PER3 = 1 + CT + 6 + 15 + 1 + 2 * CT + 1 + 7 + 7 + 1
            with dve.Fori(2, NC - 1) as c:
                it = Steps(dve, dve_s, (c - 2) * PER3 + k0)
                iteration(c, it)
                assert it.k == PER3, it.k
            own.k = k0 + (NC - 3) * PER3
            for c in range(NC - 1, NC + 2):
                iteration(c, own)

        @block.tensor
        def _(pe):
            def split3(dst, whi, wlo, mhi, mlo, start, stop):
                pe.matmul(dst, whi, mhi, start=start, stop=False)
                pe.matmul(dst, whi, mlo, start=False, stop=False)
                return pe.matmul(dst, wlo, mhi, start=False, stop=stop)

            def main1(c, p):
                r = p % R1
                pe.wait_ge(lo_ready, c * NU1 + p + 1)
                if c is 0 and p % 2 == 0:
                    pe.wait_ge(x2lo_r, p // 2 + 1)
                    pe.wait_ge(x1lo_r, p // 2 + 1)
                for b in range(2):
                    if p == 0 and c is not 0:
                        pe.wait_ge(ax_evac, 2 * c - 1 + b)
                    for t in range(U1):
                        j = p * U1 + t
                        last = split3(bank[b][:, :], xhi[b][:, j, :], xlo[b][:, j, :],
                                      ahi[r][:, t * CW:(t + 1) * CW], alo[r][:, t * CW:(t + 1) * CW],
                                      p == 0 and t == 0, p == NU1 - 1 and t == U1 - 1)
                    if p == NU1 - 1 and b == 0:
                        last.then_inc(ax0_done, 1)
                last.then_inc(unit_done, 1)

            def post1(c, p):
                if p in (0, 2, 4):
                    i = p // 2
                    if i:
                        pe.wait_ge(m_ready, 6 * c - 6 + 2 * i)
                    for b in range(2):
                        last = pe.matmul(bank[2 + b][:, :], gnnw[b][i], ms[:, b, :], start=True, stop=True)
                    last.then_inc(lay_done, 1)
                if p == 6:
                    pe.wait_ge(m_ready, 6 * c)
                    pe.wait_ge(v_done, c)
                    for t in range(CT):
                        for b in range(2):
                            last = pe.matmul(bank[4][:, t * D:(t + 1) * D], ms[:, b, t * P:(t + 1) * P], mergew[b],
                                             start=b == 0, stop=b == 1)
                    last.then_inc(merge_done, 1)
                if p == 9:
                    pe.wait_ge(z1_ready, CT * c)
                    for t in range(CT):
                        last = pe.transpose(bank[5][:, t * P:(t + 1) * P], z[:, t, :], ident[:, :])
                    last.then_inc(zT_done, 1)
                if p == 11:
                    pe.wait_ge(zT_ready, c)
                    for k in range(HB):
                        a = cols["ffn_w1"][0] + k * P
                        pe.matmul(bank[(2, 3, 6, 7)[k]][:, :], wp[:, a:a + P], zT[:, :], start=True, stop=True).then_inc(up_done, 1)
                if p == 13:
                    pe.wait_ge(h_ready, HB * c)
                    for t in range(CT):
                        for k in range(HB):
                            a = cols["ffn_w2"][0] + k * D
                            pe.matmul(bank[5][:, t * D:(t + 1) * D], hT[:, k, t * P:(t + 1) * P], wp[:, a:a + D],
                                      start=k == 0, stop=k == HB - 1)
                    for t in range(CT):
                        last = pe.matmul(bank[4][:, t:t + 1], zT[:, t * P:(t + 1) * P], W("wr"), start=True, stop=True)
                    last.then_inc(down_done, 1)

            for p in range(NU1):
                main1(0, p)
            pe.wait_ge(wp_in, 16)
            pe.wait_ge(consts, 4 + CT)
            with pe.Fori(1, NC) as c:
                for p in range(NU1):
                    main1(c, p)
                    post1(c, p)
            for p in range(NU1):
                if p == 0:
                    pe.wait_ge(ax_evac, 2 * NC)
                post1(NC, p)

            for n in range(10):
                pe.wait_ge(cnt_ready, n + 1)
                if n == 4:
                    last = pe.matmul(bank[6][:, 0:1], ones[:, :], cnt[:, 0:1], start=True, stop=True)
                elif n < 9:
                    last = pe.matmul(bank[6][:, 0:15], ones[:, :], cnt[:, :], start=True, stop=True)
                else:
                    pe.matmul(bank[6][:, 64:64 + T], before[:, :], eqc[:, 0:T], start=True, stop=True)
                    last = pe.matmul(bank[6][:, 0:T + 1], ones[:, :], eqc[:, :], start=True, stop=True)
                last.then_inc(cnt_done, 1)
            with pe.Fori(0, NC) as g:
                pe.wait_ge(z2_ready, g * CT + CT)
                for t in range(CT):
                    last = pe.transpose(bank[5][:, t * P:(t + 1) * P], z[:, t, :], ident[:, :])
                last.then_inc(z2T_done, 1)
                pe.wait_ge(z2T_ready, g + 1)
                for t in range(CT):
                    last = pe.matmul(bank[4][:, t * D:(t + 1) * D], zT[:, t * P:(t + 1) * P], W("gnnW"), start=True, stop=True)
                last.then_inc(msg_done, 1)
            pe.wait_ge(msg_ready, NC)

            def iteration(c):
                for u in range(NU2):
                    oe = expert_at(c, u)
                    new = has(c - 1, c)
                    if oe:
                        o, e = oe
                        if e == 0:
                            pe.wait_ge(zlo_ready, c)
                            if c is 1:
                                pe.wait_ge(w1_ready, 1)
                                pe.wait_ge(moe2_in, 16)
                        for k in range(HB):
                            split3(bank[1 + k][:, :], w1hi[:, e, k * P:(k + 1) * P], w1lo[:, e, k * P:(k + 1) * P],
                                   zhi[:, :], zlo[:, :], True, True).then_inc(up2_done, 1)
                    if u == 1 and new:
                        pe.wait_ge(z3_ready, CT * c)
                        for t in range(CT):
                            last = pe.transpose(bank[7][:, t * P:(t + 1) * P], z[:, t, :], ident[:, :])
                        last.then_inc(t2_done, 1)
                    if has(c, c):
                        pe.wait_ge(wt_ready, c * NU2 + u + 1)
                        if u == 0 and new:
                            pe.wait_ge(g_evac, c)
                        for t in range(U2):
                            last = pe.matmul(bank[0][:, :], VM[:, u * U2 + t, :], wt[u][:, t * CW:(t + 1) * CW],
                                             start=u == 0 and t == 0, stop=u == NU2 - 1 and t == U2 - 1)
                        last.then_inc(wt_used, 1)
                    if u == 0 and new:
                        pe.wait_ge(g_evac, c)
                        for t in range(CT):
                            last = pe.transpose(bank[6][:, t * P:(t + 1) * P], ms[:, 0, t * P:(t + 1) * P], ident[:, :])
                        last.then_inc(t1_done, 1)
                    if u == 1 and new:
                        pe.wait_ge(zhi_ready, 2 * c)
                        for t in range(CT):
                            last = pe.matmul(bank[7][:, t * E:(t + 1) * E], zT[:, t * P:(t + 1) * P], W("Wg"), start=True, stop=True)
                        last.then_inc(gate_done, 1)
                    if u == 3 and new:
                        pe.wait_ge(comb_ready, c)
                        for t in range(CT):
                            last = pe.transpose(bank[7][0:E, t * P:(t + 1) * P], comb[:, t, :], ident[:, :])
                        last.then_inc(cT_done, 1)
                    if u == 4 and new:
                        pe.wait_ge(cT_ready, c)
                        if c is 1:
                            pe.wait_ge(moeb_in, 16)
                        for t in range(CT):
                            last = pe.matmul(bank[6][:, t * D:(t + 1) * D], cTs[:, t * P:(t + 1) * P], mb2[:, :], start=True, stop=True)
                        last.then_inc(b2_done, 1)
                    if oe:
                        pe.wait_ge(h2_ready, o * (E * HB) + HB * e + HB)
                        if not (isinstance(o, int) and o == 0 and e == 0):
                            pe.wait_ge(y_used, o * E + e)
                        for t in range(CT):
                            for k in range(HB):
                                last = pe.matmul(bank[5][:, t * D:(t + 1) * D], hT[:, k, t * P:(t + 1) * P], w2[:, e, k, :],
                                                 start=k == 0, stop=k == HB - 1)
                        last.then_inc(down2_done, 1)

            iteration(0)
            iteration(1)
            with pe.Fori(2, NC - 1) as c:
                iteration(c)
            for c in range(NC - 1, NC + 2):
                iteration(c)


def kernel(**inputs):
    import numpy as np
    import concourse.bacc as bacc
    from concourse import mybir
    from concourse.bass_utils import run_bass_kernel_spmd as run

    g = {k: np.asarray(v) for k, v in inputs.items()}
    P, CW = 128, 512
    N = g["adj"].shape[0]
    adj_tiles = np.ascontiguousarray(
        g["adj"].T.reshape(N // (2 * P), 2, P, N // CW, CW).transpose(3, 0, 2, 1, 4)).reshape(-1, P, 2 * CW)

    cols, parts, at = {}, [], 0
    for name, a in (
            ("gnn0", g["L0_gnn_W1"].transpose(2, 0, 1).reshape(P, -1)),
            ("gnn1", g["L0_gnn_W2"].transpose(2, 0, 1).reshape(P, -1)),
            ("merge", g["L0_gnn_Wm"].T.reshape(2, P, P).transpose(1, 0, 2).reshape(P, -1)),
            ("gnnW", g["L1_gnn_W"]),
            ("ffn_w1", g["L0_ffn_w1"]),
            ("ffn_w2", g["L0_ffn_w2"].reshape(4, P, P).transpose(1, 0, 2).reshape(P, -1)),
            ("gnnb0", g["L0_gnn_b1"].T), ("gnnb1", g["L0_gnn_b2"].T),
            ("ffn_b1", g["L0_ffn_b1"].reshape(4, P).T),
            ("wr", g["L0_ffn_wr"]),
            ("Wg", g["L1_ffn_Wg"].T),
            ("moe_b1", g["L1_ffn_b1"].reshape(8 * 4, P).T)):
        cols[name] = (at, at + a.shape[1])
        at += a.shape[1]
        parts.append(a)
    wpack = np.ascontiguousarray(np.concatenate(parts, axis=1))
    rows, parts, at = {}, [], 0
    for name, names in (("bm", ["L0_gnn_bm"]), ("ffn_b2", ["L0_ffn_b2"]), ("B", ["L1_gnn_B"]), ("bg", ["L1_ffn_bg"]),
                        ("br", ["L0_ffn_br"]), ("eps", ["L0_gnn_eps1", "L0_gnn_eps2"])):
        a = np.concatenate([g[n] for n in names])
        rows[name] = (at, at + a.size)
        at += a.size
        parts.append(a)
    rowpack = np.concatenate(parts)[None, :]
    w1 = np.ascontiguousarray(g["L1_ffn_W1"].transpose(2, 0, 1))
    w2 = np.ascontiguousarray(g["L1_ffn_W2"].reshape(8, P, 4, P).transpose(3, 0, 2, 1))

    nc = bacc.Bacc("TRN2", target_bir_lowering=False, num_devices=1)
    arrays, args = {}, []
    for name, a in (("adj_tiles", adj_tiles), ("x", g["x"]), ("x2", g["L0_gnn_x2"]), ("wpack", wpack), ("rowpack", rowpack),
                    ("moe_w1", w1), ("moe_w2", w2), ("moe_b2", g["L1_ffn_b2"])):
        arrays[name + "_dram"] = np.ascontiguousarray(a)
        args.append(nc.dram_tensor(name + "_dram", a.shape, mybir.dt.float32, kind="ExternalInput").ap())
    args.append(nc.dram_tensor("out_dram", (N, P), mybir.dt.float32, kind="ExternalOutput").ap())
    build_program(nc, *args, cols, rows)
    return run(nc, [arrays], core_ids=[0]).results[0]["out_dram"]
```

```python
import concourse.bass as bass
from concourse import mybir
from contextlib import ExitStack


class Steps:

    def __init__(self, eng, sem, base):
        self.eng, self.sem, self.base, self.k = eng, sem, base, 0

    def do(self, ins):
        ins.then_inc(self.sem, 1)
        self.k += 1

    def wait(self):
        self.eng.wait_ge(self.sem, self.base + self.k)

    def link(self, ins):
        self.do(ins)
        self.wait()


def build_program(nc, adj_tiles, x_in, x2_in, wpack_in, rows_in, moe_w1_in, moe_w2_in, out, cols, rows):
    f32, f32r, bf16 = mybir.dt.float32, mybir.dt.float32r, mybir.dt.bfloat16
    i32, u32 = mybir.dt.int32, mybir.dt.uint32
    ALU = mybir.AluOpType
    ACT = mybir.ActivationFunctionType
    AX = mybir.AxisListType.X
    ds = bass.ds

    N, D = x_in.shape
    P = 128
    T = N // P
    CW = 512
    NC = N // CW
    CT = CW // P
    U1 = 2
    NU1 = T // U1
    T0 = 8
    U2 = 4
    NU2 = T // U2
    E = moe_w1_in.shape[1]
    HB = 4
    KEEP = N // 2 - 1
    EPS = 1e-5
    A1, R1 = 8, 4
    LAG = 3
    TINY = 1e-18
    assert NU2 == E == 8 and NU1 == 16

    x_v = x_in.rearrange("(t p) d -> p t d", p=P)
    x2_v = x2_in.rearrange("(t p) d -> p t d", p=P)
    out_v = out.rearrange("(c t p) d -> c p t d", t=CT, p=P)

    ctx = ExitStack()
    with ctx:
        def sb(name, shape, dt=f32):
            return ctx.enter_context(nc.sbuf_tensor(name, shape, dt))

        def sem(name):
            return ctx.enter_context(nc.semaphore(name))

        wp = sb("wp", [P, wpack_in.shape[1]])
        rw = sb("rw", [P, rows_in.shape[1]])
        ident = sb("ident", [P, P])
        ones = sb("ones", [P, P])
        before = sb("before", [P, P])
        XU = sb("XU", [P, T, D])
        VM = sb("VM", [P, T, D])
        ms = sb("ms", [P, 2, CW])
        hT = sb("hT", [P, HB, CW])
        z = sb("z", [P, CT, D])
        zT = sb("zT", [P, CW])
        x3 = sb("x3", [P, CT, D])
        outt = sb("outt", [P, CT, D])
        nmr = sb("nmr", [P, T])
        bn6 = sb("bn6", [P, T, 6])
        mv = sb("mv", [P, T, 2])
        rs_v = sb("rs_v", [P, T])
        rs_y = sb("rs_y", [P, T])
        rs_t = sb("rs_t", [P, T])
        scale12 = sb("scale12", [P, 2])
        cb = sb("cb", [P, 2])
        wtok = sb("wtok", [P, T])
        key = sb("key", [P, T], i32)
        keyt = sb("keyt", [P, T], i32)
        khi = sb("khi", [P, T])
        klo = sb("klo", [P, T])
        steps15 = sb("steps15", [P, 15])
        steps15i = sb("steps15i", [P, 15], i32)
        thr = sb("thr", [P, 15])
        cmp = sb("cmp", [P, 15, T])
        cnt = sb("cnt", [P, 15])
        digit = sb("digit", [P, 1])
        Thi = sb("Thi", [P, 1])
        Tlo = sb("Tlo", [P, 1])
        kleft = sb("kleft", [P, 1])
        above = sb("above", [P, T])
        eqc = sb("eqc", [P, T + 1])
        tots = sb("tots", [P, T])
        rank = sb("rank", [P, T])
        sel = sb("sel", [P, T])
        gate = sb("gate", [P, CT, E])
        top8 = sb("top8", [P, CT, E])
        top8i = sb("top8i", [P, CT, E], u32)
        topf = sb("topf", [P, CT, E])
        iota8 = sb("iota8", [P, CT, E])
        iota8i = sb("iota8i", [P, E], i32)
        pd = sb("pd", [P, CT])
        pe2 = sb("pe2", [P, CT])
        ps1 = sb("ps1", [P, CT])
        prob = sb("prob", [P, 2, CT])
        hot = sb("hot", [P, CT, E])
        gap = sb("gap", [P, 1])
        comb = sb("comb", [P, CT, E])
        combr = sb("combr", [P, CT, E], f32r)
        comb2 = sb("comb2", [P, CT, 2 * E])

        first = ExitStack()
        raw = [first.enter_context(nc.sbuf_tensor(f"raw{s}", [P, U1 * CW], f32)) for s in range(A1)]
        ahi = [first.enter_context(nc.sbuf_tensor(f"ahi{s}", [P, U1 * CW], f32r)) for s in range(R1)]
        alo = [first.enter_context(nc.sbuf_tensor(f"alo{s}", [P, U1 * CW], f32r)) for s in range(R1)]
        xhi = [first.enter_context(nc.sbuf_tensor(f"xhi{b}", [P, T, D], f32r)) for b in range(2)]
        xlo = [first.enter_context(nc.sbuf_tensor(f"xlo{b}", [P, T, D], f32r)) for b in range(2)]
        first.close()
        wt = [sb(f"wt{u}", [P, U2 * CW]) for u in range(NU2)]
        w1hi = sb("w1hi", [P, E, HB * P], f32r)
        w1lo = sb("w1lo", [P, E, HB * P], f32r)
        w2 = sb("w2", [P, E, HB, D])
        zhi = sb("zhi", [P, CW], f32r)
        zlo = sb("zlo", [P, CW], f32r)
        scaled = sb("scaled", [P, CW])
        acc = sb("acc", [P, CW])
        cbs = sb("cbs", [P, CW])
        cTs = sb("cTs", [2 * E, CW], f32r)
        pick = sb("pick", [2 * E, E, P], f32r)
        pickf = sb("pickf", [2 * E, E, P])

        bank = [ctx.enter_context(nc.psum_tensor(f"bank{i}", [P, 512], f32)) for i in range(8)]

        def W(name):
            a, b = cols[name]
            return wp[:, a:b]

        def R(name):
            a, b = rows[name]
            return rw[:, a:b]

        gnnw = [[wp[:, cols[f"gnn{b}"][0] + D * i:cols[f"gnn{b}"][0] + D * (i + 1)] for i in range(3)] for b in range(2)]
        mergew = [wp[:, cols["merge"][0] + D * b:cols["merge"][0] + D * (b + 1)] for b in range(2)]

        x_in_s, x2_in_s, wp_in, rw_in = sem("x_loaded"), sem("x2_loaded"), sem("wp_loaded"), sem("rows_loaded")
        adj_in = [sem(f"adj_in{s}") for s in range(A1)]
        w_in = [sem(f"wt_in{u}") for u in range(NU2)]
        moe1_in, moe2_in = sem("moe_w1_in"), sem("moe_w2_in")
        x8_in_s = sem("x_first_loaded")
        nmr_ready, z2T_done = sem("nmr_ready"), sem("z2T_done")
        stored = sem("stored")
        consts = sem("consts")
        consts_v = sem("consts_v")
        x2hi_r, x2lo_r, xn_r, x1hi_r, x1lo_r = sem("x2hi"), sem("x2lo"), sem("xn"), sem("x1hi"), sem("x1lo")
        hi_ready, lo_ready, unit_done = sem("hi_ready"), sem("lo_ready"), sem("unit_done")
        ax0_done, ax_evac, lay_done, m_ready = sem("ax0_done"), sem("ax_evac"), sem("lay_done"), sem("m_ready")
        merge_done, z1_ready, zT_done, zT_ready = sem("merge_done"), sem("z1_ready"), sem("zT_done"), sem("zT_ready")
        up_done, h_ready, down_done, v_done = sem("up_done"), sem("h_ready"), sem("down_done"), sem("v_done")
        cnt_ready, cnt_done = sem("cnt_ready"), sem("cnt_done")
        z2_ready, z2T_ready, msg_done, msg_ready = sem("z2_ready"), sem("z2T_ready"), sem("msg_done"), sem("msg_ready")
        msk_ready, ln_done, rec_done, q_ready, wt_ready, wt_used = sem("msk_ready"), sem("ln_done"), sem("rec_done"), sem("q_ready"), sem("wt_ready"), sem("wt_used")
        w1_ready = sem("w1_ready")
        g_evac, t1_done, z3_ready, t2_done, zhi_ready, zlo_ready = sem("g_evac"), sem("t1_done"), sem("z3_ready"), sem("t2_done"), sem("zhi_ready"), sem("zlo_ready")
        gate_done, diff_ready, exp_ready, comb_ready, cT_done, cT_ready, zT2_ready = sem("gate_done"), sem("diff_ready"), sem("exp_ready"), sem("comb_ready"), sem("cT_done"), sem("cT_ready"), sem("zT2_ready")
        cb_done, cb_ready, final_done, out_ready = sem("cb_done"), sem("cb_ready"), sem("final_done"), sem("out_ready")
        up2_done, h2a_ready, h2v_ready, down2_done, y_used, acc_done = sem("up2_done"), sem("h2a_ready"), sem("h2v_ready"), sem("down2_done"), sem("y_used"), sem("acc_done")
        dve_s, pool_s = sem("dve_steps"), sem("pool_steps")

        block = ctx.enter_context(nc.Block())

        ALL1 = NC * NU1

        def has(chunk, c):
            return not isinstance(c, int) or 0 <= chunk < NC

        def expert_at(c, u):
            o, e = (c - 2, E - LAG + u) if u < LAG else (c - 1, u - LAG)
            return (o, e) if has(o, c) else None

        @block.sync
        def _(sp):
            sp.dma_start(XU[:, 0:T0, :], x_v[:, 0:T0, :]).then_inc(x8_in_s, 16)
            sp.dma_start(VM[:, :, :], x2_v).then_inc(x2_in_s, 16)
            sp.dma_start(XU[:, T0:T, :], x_v[:, T0:T, :]).then_inc(x_in_s, 16)
            sp.dma_start(rw[:, :], rows_in[0, :].partition_broadcast(P)).then_inc(rw_in, 16)

            def load1(c, p, off):
                if not isinstance(c, int) or c * NU1 + p >= A1:
                    sp.wait_ge(lo_ready, c * NU1 + p - (A1 - 1))
                sp.dma_start(raw[p % A1][:, :], adj_tiles[off, :, :]).then_inc(adj_in[p % A1], 16)

            for p in range(NU1):
                load1(0, p, p)
                if p == 3:
                    sp.dma_start(wp[:, :], wpack_in[:, :]).then_inc(wp_in, 16)
            with sp.Fori(1, NC) as c:
                for p in range(NU1):
                    off = sp.snap(c * NU1 + p)
                    sp.wait_ge(lo_ready, c * NU1 + p - (A1 - 1))
                    sp.dma_start(raw[p % A1][:, :].rearrange("p (a f) -> p a f", a=1),
                                 adj_tiles[ds(off, 1), :, :].rearrange("a p f -> p a f")).then_inc(adj_in[p % A1], 16)

            sp.wait_ge(unit_done, ALL1)

            def load2(cc, u):
                src = adj_tiles[ds(cc * NU1 + 2 * u, 2), :, :] if not isinstance(cc, int) else adj_tiles[cc * NU1 + 2 * u:cc * NU1 + 2 * u + 2, :, :]
                return sp.dma_start(wt[u][:, :].rearrange("p (a f) -> p a f", a=2), src.rearrange("a p f -> p a f")).then_inc(w_in[u], 16)

            for u in range(NU2):
                load2(0, u)
                if u == 3:
                    sp.wait_ge(down_done, NC)
                    sp.dma_start(hT[:, :, :], moe_w1_in[:, 0:E // 2, :]).then_inc(moe1_in, 16)
            sp.dma_start(w2[:, :, :, :], moe_w2_in[:, :, :, :]).then_inc(moe2_in, 16)

            sp.wait_ge(w1_ready, 3)
            sp.dma_start(hT[:, :, :], moe_w1_in[:, E // 2:E, :]).then_inc(moe1_in, 16)

            def store(o, ro):
                sp.wait_ge(out_ready, o + 1)
                dst = out_v[o, :, :, :] if isinstance(o, int) else out_v[ds(ro, 1), :, :, :].rearrange("a p t d -> p (a t) d")
                sp.dma_start(dst, outt[:, :, :]).then_inc(stored, 16)

            def iteration(c):
                for u in range(NU2):
                    if not isinstance(c, int):
                        off = sp.snap(c * NU1 + NU1 + 2 * u)
                        sp.wait_ge(wt_used, c * NU2 + u + 1)
                        sp.dma_start(wt[u][:, :].rearrange("p (a f) -> p a f", a=2),
                                     adj_tiles[ds(off, 2), :, :].rearrange("a p f -> p a f")).then_inc(w_in[u], 16)
                    elif c + 1 < NC:
                        sp.wait_ge(wt_used, c * NU2 + u + 1)
                        load2(c + 1, u)
                    if u == 4 and has(c - 2, c):
                        store(c - 2, None if isinstance(c, int) else sp.snap(c - 2))

            iteration(0)
            iteration(1)
            with sp.Fori(2, NC - 1) as c:
                iteration(c)
            for c in range(NC - 1, NC + 2):
                iteration(c)
            sp.wait_ge(stored, 16 * NC)

        @block.gpsimd
        def _(pool):
            own = Steps(pool, pool_s, 0)
            own.do(pool.memset(ident[:, :], 0.0))
            pool.memset(ones[:, :], 1.0).then_inc(consts, 1)
            own.do(pool.memset(before[:, :], 1.0))
            own.do(pool.iota(steps15i[:, :], pattern=[[1, 15]], base=1, channel_multiplier=0))
            own.do(pool.iota(iota8i[:, :], pattern=[[1, E]], base=0, channel_multiplier=0))
            own.wait()
            pool.affine_select(out=ident[:, :], in_=ident[:, :], compare_op=ALU.not_equal, fill=1.0, base=0,
                               pattern=[[-1, P]], channel_multiplier=1).then_inc(consts, 1)
            pool.affine_select(out=before[:, :], in_=before[:, :], compare_op=ALU.is_ge, fill=0.0, base=-1,
                               pattern=[[1, P]], channel_multiplier=-1).then_inc(consts, 1)
            pool.tensor_copy(steps15[:, :], steps15i[:, :]).then_inc(consts, 1)
            for t in range(CT):
                pool.tensor_copy(iota8[:, t, :], iota8i[:, :]).then_inc(consts, 1)
            for g in range(NC):
                s = slice(g * CT, (g + 1) * CT)
                pool.wait_ge(x2hi_r, g + 1)
                pool.tensor_tensor(xlo[1][:, s, :], VM[:, s, :], xhi[1][:, s, :].bitcast(f32), ALU.subtract).then_inc(x2lo_r, 1)
            pool.wait_ge(unit_done, ALL1)
            own.link(pool.memset(pickf[:, :, :], 0.0))
            for first_k in (0, E):
                own.link(pool.affine_select(out=pickf[:, :, :], in_=pickf[:, :, :], compare_op=ALU.not_equal, fill=1.0,
                                            base=-first_k, pattern=[[-1, E], [0, P]], channel_multiplier=1))
            pool.tensor_copy(pick[:, :, :], pickf[:, :, :]).then_inc(w1_ready, 1)
            for h in range(2):
                s = slice(h * E // 2, (h + 1) * E // 2)
                pool.wait_ge(moe1_in, 16 * (h + 1))
                pool.tensor_copy(w1hi[:, s, :], hT[:, :, :]).then_inc(w1_ready, 1)
                pool.wait_ge(w1_ready, 2 * h + 2)
                pool.tensor_tensor(w1lo[:, s, :], hT[:, :, :], w1hi[:, s, :].bitcast(f32), ALU.subtract).then_inc(w1_ready, 1)

        @block.scalar
        def _(act):
            act.wait_ge(x2_in_s, 16)
            for g in range(NC):
                s = slice(g * CT, (g + 1) * CT)
                act.activation(xhi[1][:, s, :], VM[:, s, :], ACT.Copy).then_inc(x2hi_r, 1)

            def hi(c, p):
                act.wait_ge(adj_in[p % A1], 16 * (2 * c + p // A1 + 1))
                if not isinstance(c, int) or c * NU1 + p >= R1:
                    act.wait_ge(unit_done, c * NU1 + p - (R1 - 1))
                act.activation(ahi[p % R1][:, :], raw[p % A1][:, :], ACT.Copy).then_inc(hi_ready, 1)

            def first_pass(c, main, post):
                for p in range(NU1):
                    if c is 0 and p % 2 == 0:
                        g = p // 2
                        act.wait_ge(xn_r, CT * (g + 1))
                        act.activation(xhi[0][:, g * CT:(g + 1) * CT, :], hT[:, g % 4, :], ACT.Copy).then_inc(x1hi_r, 1)
                    if main and p != 3:
                        hi(c, p)
                    if post and p == 2:
                        act.wait_ge(ax0_done, c)
                        act.activation(ms[:, 0, :], bank[0][:, :], ACT.Copy, scale=scale12[:, 0:1]).then_inc(ax_evac, 1)
                        act.wait_ge(unit_done, c * NU1)
                        act.activation(ms[:, 1, :], bank[1][:, :], ACT.Copy, scale=scale12[:, 1:2]).then_inc(ax_evac, 1)
                    if main and p == 3:
                        hi(c, p)
                    if post and p in (3, 5, 7):
                        i = (p - 3) // 2
                        act.wait_ge(lay_done, 3 * c - 3 + i + 1)
                        for b in range(2):
                            a = cols[f"gnnb{b}"][0] + i
                            act.activation(ms[:, b, :], bank[2 + b][:, :], ACT.Relu, bias=wp[:, a:a + 1]).then_inc(m_ready, 1)
                    if post and p == 12:
                        act.wait_ge(zT_done, c)
                        act.activation(zT[:, :], bank[5][:, :], ACT.Copy).then_inc(zT_ready, 1)
                    if post and p == 14:
                        for k in range(HB):
                            a = cols["ffn_b1"][0] + k
                            act.wait_ge(up_done, HB * c - HB + k + 1)
                            act.activation(hT[:, k, :], bank[(2, 3, 6, 7)[k]][:, :], ACT.Gelu_apprx_tanh,
                                           bias=wp[:, a:a + 1]).then_inc(h_ready, 1)

            first_pass(0, True, False)
            with act.Fori(1, NC) as c:
                first_pass(c, True, True)
            first_pass(NC, False, True)

            def ln(cc, u):
                act.wait_ge(msk_ready, cc * NU2 + u + 1)
                act.activation(wt[u][:, :], wt[u][:, :], ACT.Ln, bias=cb[:, 0:1]).then_inc(ln_done, 1)

            def rec(cc, u):
                act.wait_ge(ln_done, cc * NU2 + u + 1)
                act.activation(wt[u][:, :], wt[u][:, :], ACT.Exp, scale=-1.0).then_inc(rec_done, 1)

            def sens(cc, u):
                act.wait_ge(q_ready, cc * NU2 + u + 1)
                act.activation(wt[u][:, :], wt[u][:, :], ACT.Exp, scale=-2.0, bias=cb[:, 1:2]).then_inc(wt_ready, 1)

            for u in range(4):
                ln(0, u)
            for u in range(4):
                rec(0, u)
            for u in range(4):
                sens(0, u)

            act.wait_ge(nmr_ready, 1)
            with act.Fori(0, NC // 2) as i:
                for b in range(2):
                    for k in range(CT):
                        t = i * (2 * CT) + b * CT + k
                        act.activation((z, outt)[b][:, k:k + 1, :], XU[:, ds(t, 1), :], ACT.Identity, bias=nmr[:, ds(t, 1)],
                                       scale=rs_y[:, ds(t, 1)]).then_inc(z2_ready, 1)
                for b in range(2):
                    act.wait_ge(z2T_done, 2 * i + b + 1)
                    act.activation((zT[:, :], ms[:, 0, :])[b], bank[5 + b][:, :], ACT.Copy).then_inc(z2T_ready, 1)

            def iteration(c):
                new = has(c - 1, c)
                for u in range(NU2):
                    if u == 0 and new:
                        act.wait_ge(wt_used, c * NU2)
                        act.activation(ms[:, 0, :], bank[0][:, :], ACT.Copy).then_inc(g_evac, 1)
                    if (oe := expert_at(c, u)):
                        o, e = oe
                        for k in range(HB // 2):
                            a = cols["moe_b1"][0] + HB * e + k
                            act.wait_ge(up2_done, o * (E * HB) + HB * e + k + 1)
                            act.activation(hT[:, k, :], bank[1 + k][:, :], ACT.Relu, bias=wp[:, a:a + 1]).then_inc(h2a_ready, 1)
                        act.wait_ge(cb_done, o * E + e + 1)
                        if not (isinstance(o, int) and o == 0 and e == 0):
                            act.wait_ge(y_used, o * E + e)
                        act.activation(cbs[:, :], bank[7][:, :], ACT.Copy).then_inc(cb_ready, 1)
                    if u == 1 and new:
                        act.wait_ge(t2_done, c)
                        act.activation(zT[:, :], bank[6][:, :], ACT.Copy).then_inc(zT2_ready, 1)
                    if u == 2 and new:
                        act.wait_ge(zT2_ready, c)
                        act.activation(zhi[:, :], zT[:, :], ACT.Copy).then_inc(zhi_ready, 1)
                        act.wait_ge(diff_ready, c)
                        act.activation(pe2[:, :], pd[:, :], ACT.Exp).then_inc(exp_ready, 1)
                    half, k = u // 4, u % 4
                    if has(c + half, c):
                        cc, b = c + half, 4 * (1 - half)
                        for fn, j in (((ln, 0), (ln, 1), (ln, 2)), ((ln, 3), (rec, 0), (rec, 1)),
                                      ((rec, 2), (rec, 3), (sens, 0)), ((sens, 1), (sens, 2), (sens, 3)))[k]:
                            fn(cc, b + j)
                    if u == 2 and new:
                        act.wait_ge(cT_done, c)
                        act.activation(cTs[:, :], bank[6][0:2 * E, :], ACT.Copy).then_inc(cT_ready, 1)

            iteration(0)
            iteration(1)
            with act.Fori(2, NC - 1) as c:
                iteration(c)
            for c in range(NC - 1, NC + 2):
                iteration(c)

        @block.vector
        def _(dve):
            own = Steps(dve, dve_s, 0)

            def rsqrt(own, var, n):
                v, y, t = rs_v[:, 0:n], rs_y[:, 0:n], rs_t[:, 0:n]
                own.link(dve.tensor_scalar(v, var, EPS, None, ALU.add))
                own.link(dve.tensor_scalar(t.bitcast(i32), v.bitcast(i32), 1, None, ALU.logical_shift_right))
                own.link(dve.tensor_scalar(y.bitcast(i32), t.bitcast(i32), -1.0, 1597463007.0, ALU.mult, ALU.add))
                for _ in range(4):
                    own.link(dve.scalar_tensor_tensor(out=t, in0=y, scalar=0.5, in1=y, op0=ALU.mult, op1=ALU.mult))
                    own.link(dve.tensor_tensor(t, t, v, ALU.mult))
                    own.link(dve.scalar_tensor_tensor(out=y, in0=t, scalar=1.5, in1=y, op0=ALU.subtract, op1=ALU.mult))

            def moments(own, n):
                b, m, v = bn6[:, 0:n, :], mv[:, 0:n, 0], mv[:, 0:n, 1]
                own.do(dve.tensor_tensor(m, b[:, :, 1], b[:, :, 4], ALU.add))
                own.do(dve.tensor_tensor(rs_t[:, 0:n], b[:, :, 2], b[:, :, 5], ALU.add))
                own.link(dve.tensor_tensor(rs_y[:, 0:n], b[:, :, 1], b[:, :, 4], ALU.subtract))
                own.do(dve.tensor_scalar(m, m, 0.5, None, ALU.mult))
                own.link(dve.scalar_tensor_tensor(out=rs_y[:, 0:n], in0=rs_y[:, 0:n], scalar=0.25, in1=rs_y[:, 0:n],
                                                  op0=ALU.mult, op1=ALU.mult))
                own.link(dve.scalar_tensor_tensor(out=v, in0=rs_t[:, 0:n], scalar=1.0 / D, in1=rs_y[:, 0:n],
                                                  op0=ALU.mult, op1=ALU.add))

            def stats(own, src, n):
                for k in range(n):
                    own.do(dve.bn_stats(bn6[:, k, :], src(k)))
                own.wait()
                moments(own, n)

            own.do(dve.memset(cb[:, 0:1], TINY))
            own.do(dve.memset(cb[:, 1:2], -2.0))
            dve.wait_ge(x8_in_s, 16)
            stats(own, lambda k: XU[:, k, :], T0)
            rsqrt(own, mv[:, 0:T0, 1], T0)
            dve.wait_ge(rw_in, 16)
            dve.tensor_scalar(scale12[:, :], R("eps"), 1.0, 1.0, ALU.add, ALU.add).then_inc(consts_v, 1)

            def lo(c, p):
                dve.wait_ge(hi_ready, c * NU1 + p + 1)
                dve.tensor_tensor(alo[p % R1][:, :], raw[p % A1][:, :], ahi[p % R1][:, :].bitcast(f32), ALU.subtract).then_inc(lo_ready, 1)

            def norm_x(g):
                if g * CT == T0:
                    dve.wait_ge(x_in_s, 16)
                    stats(own, lambda k: XU[:, T0 + k, :], T - T0)
                    rsqrt(own, mv[:, 0:T - T0, 1], T - T0)
                if g >= 4:
                    dve.wait_ge(x1lo_r, g - 3)
                    dve.wait_ge(x1hi_r, g - 3)
                for k in range(CT):
                    t = g * CT + k
                    m = t if t < T0 else t - T0
                    dve.tensor_scalar(hT[:, g % 4, k * D:(k + 1) * D], XU[:, t, :], mv[:, m, 0:1], rs_y[:, m:m + 1],
                                      ALU.subtract, ALU.mult).then_inc(xn_r, 1)
                dve.wait_ge(x1hi_r, g + 1)
                dve.tensor_tensor(xlo[0][:, g * CT:(g + 1) * CT, :], hT[:, g % 4, :],
                                  xhi[0][:, g * CT:(g + 1) * CT, :].bitcast(f32), ALU.subtract).then_inc(x1lo_r, 1)

            def tiles(c, back):
                return slice((c - back) * CT, (c - back + 1) * CT) if isinstance(c, int) else ds((c - back) * CT, CT)

            def mask(cc, u):
                dve.wait_ge(w_in[u], 16 * (cc + 1))
                dve.scalar_tensor_tensor(out=wt[u][:, :], in0=wt[u][:, :], scalar=1.0, in1=wt[u][:, :],
                                         op0=ALU.is_lt, op1=ALU.mult).then_inc(msk_ready, 1)

            def square(cc, u):
                dve.wait_ge(rec_done, cc * NU2 + u + 1)
                dve.scalar_tensor_tensor(out=wt[u][:, :], in0=wt[u][:, :], scalar=2.0, in1=wt[u][:, :],
                                         op0=ALU.subtract, op1=ALU.mult).then_inc(q_ready, 1)

            def first_pass(c, main, post, own):
                for p in range(NU1):
                    if c is 0 and p % 2 == 0:
                        norm_x(p // 2)
                    if main:
                        lo(c, p)
                    if post and p == 10:
                        u = XU[:, tiles(c, 1), :]
                        dve.wait_ge(merge_done, c)
                        own.link(dve.tensor_tensor(x3[:, :, :], bank[4][:, :].rearrange("p (t d) -> p t d", t=CT), u, ALU.add))
                        stats(own, lambda k: x3[:, k, :], CT)
                        rsqrt(own, mv[:, 0:CT, 1], CT)
                        for k in range(CT):
                            dve.tensor_scalar(z[:, k, :], x3[:, k, :], mv[:, k, 0:1], rs_y[:, k:k + 1], ALU.subtract, ALU.mult).then_inc(z1_ready, 1)
                        dve.wait_ge(z1_ready, CT * c)
                        own.link(dve.tensor_tensor(u, x3[:, :, :], z[:, :, :], ALU.add))
                    if post and not main and p == 15:
                        for u in range(4):
                            mask(0, u)
                    if post and p == 15:
                        y = VM[:, tiles(c, 1), :]
                        wv = wtok[:, tiles(c, 1)]
                        dve.wait_ge(down_done, c)
                        own.do(dve.tensor_tensor(wv, bank[4][:, 0:CT], R("br").to_broadcast([P, CT]), ALU.add))
                        own.link(dve.tensor_tensor(y, bank[5][:, :].rearrange("p (t d) -> p t d", t=CT),
                                                   R("ffn_b2").unsqueeze(1).to_broadcast([P, CT, D]), ALU.add))
                        dve.tensor_tensor(y, y, wv.unsqueeze(2).to_broadcast([P, CT, D]), ALU.mult).then_inc(v_done, 1)

            PER1 = 1 + CT + 6 + 15 + 1 + 2
            first_pass(0, True, False, own)
            dve.tensor_tensor(XU[:, :, :], XU[:, :, :], R("bm").unsqueeze(1).to_broadcast([P, T, D]), ALU.add).then_inc(v_done, 1)
            dve.wait_ge(v_done, 1)
            k0 = own.k
            with dve.Fori(1, NC) as c:
                it = Steps(dve, dve_s, (c - 1) * PER1 + k0)
                first_pass(c, True, True, it)
                assert it.k == PER1, it.k
            own.k = k0 + (NC - 1) * PER1

            first_pass(NC, False, True, own)

            dve.wait_ge(consts, 4 + CT)
            dve.wait_ge(v_done, NC + 1)
            own.link(dve.tensor_scalar(keyt[:, :], wtok[:, :].bitcast(i32), 31, -2147483648, ALU.arith_shift_right, ALU.bitwise_or))
            own.link(dve.tensor_tensor(key[:, :], wtok[:, :].bitcast(i32), keyt[:, :], ALU.bitwise_xor))
            own.link(dve.tensor_scalar(keyt[:, :], key[:, :], 16, None, ALU.logical_shift_right))
            own.link(dve.tensor_copy(khi[:, :], keyt[:, :]))
            own.link(dve.tensor_scalar(key[:, :], key[:, :], 65535, None, ALU.bitwise_and))
            own.link(dve.tensor_copy(klo[:, :], key[:, :]))
            own.do(dve.memset(Thi[:, :], 0.0))
            own.do(dve.memset(Tlo[:, :], 1.0))
            own.link(dve.memset(kleft[:, :], float(KEEP)))
            asked = [0]

            def count(ins):
                ins.then_inc(cnt_ready, 1)
                asked[0] += 1
                dve.wait_ge(cnt_done, asked[0])

            def search(vals, t_ap):
                for shift in (12, 8, 4, 0):
                    own.link(dve.tensor_scalar(thr[:, :], steps15[:, :], float(1 << shift), t_ap, ALU.mult, ALU.add))
                    own.link(dve.tensor_tensor(cmp[:, :, :], vals.unsqueeze(1).to_broadcast([P, 15, T]),
                                               thr[:, :].unsqueeze(2).to_broadcast([P, 15, T]), ALU.is_ge))
                    count(dve.tensor_reduce(out=cnt[:, :], in_=cmp[:, :, :], op=ALU.add, axis=AX))
                    own.link(dve.tensor_scalar(thr[:, :], bank[6][:, 0:15], kleft[:, :], None, ALU.is_ge))
                    own.link(dve.tensor_reduce(out=digit[:, :], in_=thr[:, :], op=ALU.add, axis=AX))
                    own.link(dve.scalar_tensor_tensor(out=t_ap, in0=digit[:, :], scalar=float(1 << shift), in1=t_ap,
                                                      op0=ALU.mult, op1=ALU.add))

            search(khi[:, :], Thi[:, :])
            own.link(dve.tensor_scalar(above[:, :], khi[:, :], Thi[:, :], None, ALU.is_gt))
            count(dve.tensor_reduce(out=cnt[:, 0:1], in_=above[:, :], op=ALU.add, axis=AX))
            own.do(dve.tensor_scalar(kleft[:, :], bank[6][:, 0:1], -1.0, float(KEEP), ALU.mult, ALU.add))
            own.link(dve.tensor_scalar(klo[:, :], klo[:, :], 1.0, None, ALU.add))
            own.link(dve.scalar_tensor_tensor(out=klo[:, :], in0=khi[:, :], scalar=Thi[:, :], in1=klo[:, :],
                                              op0=ALU.is_equal, op1=ALU.mult))
            search(klo[:, :], Tlo[:, :])
            own.do(dve.scalar_tensor_tensor(out=above[:, :], in0=klo[:, :], scalar=Tlo[:, :], in1=above[:, :],
                                            op0=ALU.is_gt, op1=ALU.add))
            own.link(dve.tensor_scalar(eqc[:, 0:T], klo[:, :], Tlo[:, :], None, ALU.is_equal))
            count(dve.tensor_reduce(out=eqc[:, T:T + 1], in_=above[:, :], op=ALU.add, axis=AX))
            own.do(dve.tensor_scalar(kleft[:, :], bank[6][:, T:T + 1], -1.0, float(KEEP), ALU.mult, ALU.add))
            own.link(dve.tensor_copy(rank[:, :], bank[6][:, 0:T]))
            own.link(dve.tensor_tensor_scan(tots[:, :], ones[:, 0:T], rank[:, :], 0.0, ALU.mult, ALU.add))
            own.link(dve.tensor_tensor(tots[:, :], tots[:, :], rank[:, :], ALU.subtract))
            own.link(dve.tensor_tensor(rank[:, :], bank[6][:, 64:64 + T], tots[:, :], ALU.add))
            own.link(dve.scalar_tensor_tensor(out=sel[:, :], in0=rank[:, :], scalar=kleft[:, :], in1=eqc[:, 0:T],
                                              op0=ALU.is_lt, op1=ALU.mult))
            own.link(dve.tensor_tensor(sel[:, :], sel[:, :], above[:, :], ALU.add))

            G = 2 * CT
            k0 = own.k
            with dve.Fori(0, T // G) as g:
                it = Steps(dve, dve_s, g * G + k0)
                for k in range(G):
                    t = g * G + k
                    it.do(dve.scalar_tensor_tensor(out=XU[:, ds(t, 1), :], in0=VM[:, ds(t, 1), :], scalar=sel[:, ds(t, 1)],
                                                   in1=XU[:, ds(t, 1), :], op0=ALU.mult, op1=ALU.add))
            own.k = k0 + T
            own.wait()
            k0 = own.k
            with dve.Fori(0, T // G) as g:
                it = Steps(dve, dve_s, g * G + k0)
                for k in range(G):
                    it.do(dve.bn_stats(bn6[:, ds(g * G + k, 1), :], XU[:, ds(g * G + k, 1), :]))
            own.k = k0 + T
            own.wait()
            moments(own, T)
            rsqrt(own, mv[:, :, 1], T)
            dve.scalar_tensor_tensor(out=nmr[:, :], in0=mv[:, :, 0], scalar=-1.0, in1=rs_y[:, 0:T],
                                     op0=ALU.mult, op1=ALU.mult).then_inc(nmr_ready, 1)
            for u in range(4):
                square(0, u)
            for b in range(2):
                dve.memset(gap[:, :], 0.0).then_inc(msg_ready, 1)
                dve.wait_ge(msg_ready, b + 1)
            with dve.Fori(0, NC // 2) as i:
                for b in range(2):
                    dve.wait_ge(msg_done, 2 * i + b + 1)
                    dve.tensor_tensor(VM[:, ds(i * (2 * CT) + b * CT, CT), :], bank[3 + b][:, :].rearrange("p (t d) -> p t d", t=CT),
                                      R("B").unsqueeze(1).to_broadcast([P, CT, D]), ALU.add).then_inc(msg_ready, 1)
            mask(0, 4)
            mask(0, 5)

            def chunk_norm(c, own):
                dve.wait_ge(t1_done, c)
                own.link(dve.tensor_tensor(x3[:, :, :], bank[6][:, :].rearrange("p (t d) -> p t d", t=CT),
                                           XU[:, tiles(c, 1), :], ALU.add))
                stats(own, lambda k: x3[:, k, :], CT)
                rsqrt(own, mv[:, 0:CT, 1], CT)
                for k in range(CT):
                    dve.tensor_scalar(z[:, k, :], x3[:, k, :], mv[:, k, 0:1], rs_y[:, k:k + 1],
                                      ALU.subtract, ALU.mult).then_inc(z3_ready, 1)
                own.do(dve.tensor_copy(XU[:, tiles(c, 1), :], x3[:, :, :]))

            def choose(c, own):
                dve.wait_ge(gate_done, c)
                own.link(dve.tensor_tensor(gate[:, :, :], bank[6][:, 0:CT * E].rearrange("p (t e) -> p t e", t=CT),
                                           R("bg").unsqueeze(1).to_broadcast([P, CT, E]), ALU.add))
                dve.memset(gap[:, :], 0.0)
                for t in range(CT):
                    own.do(dve.max(top8[:, t, :], gate[:, t, :]))
                own.wait()
                dve.tensor_tensor(pd[:, :], top8[:, :, 1], top8[:, :, 0], ALU.subtract).then_inc(diff_ready, 1)
                for t in range(CT):
                    own.do(dve.max_index(top8i[:, t, :], top8[:, t, :], gate[:, t, :]))
                own.wait()
                own.link(dve.tensor_copy(topf[:, :, :], top8i[:, :, :]))

            def combine_weights(c, own):
                dve.wait_ge(exp_ready, c)
                own.link(dve.tensor_scalar(ps1[:, :], pe2[:, :], 1.0, None, ALU.add))
                own.link(dve.reciprocal(prob[:, 0, :], ps1[:, :]))
                own.link(dve.tensor_tensor(prob[:, 1, :], pe2[:, :], prob[:, 0, :], ALU.mult))
                own.do(dve.tensor_tensor(hot[:, :, :], iota8[:, :, :], topf[:, :, 0:1].to_broadcast([P, CT, E]), ALU.is_equal))
                own.link(dve.tensor_tensor(comb[:, :, :], iota8[:, :, :], topf[:, :, 1:2].to_broadcast([P, CT, E]), ALU.is_equal))
                own.do(dve.tensor_tensor(hot[:, :, :], hot[:, :, :], prob[:, 0, :].unsqueeze(2).to_broadcast([P, CT, E]), ALU.mult))
                own.link(dve.tensor_tensor(comb[:, :, :], comb[:, :, :], prob[:, 1, :].unsqueeze(2).to_broadcast([P, CT, E]), ALU.mult))
                own.link(dve.tensor_tensor(comb[:, :, :], comb[:, :, :], hot[:, :, :], ALU.add))
                own.link(dve.tensor_copy(combr[:, :, :], comb[:, :, :]))
                dve.tensor_copy(comb2[:, :, 0:E], combr[:, :, :].bitcast(f32)).then_inc(comb_ready, 1)
                dve.tensor_tensor(comb2[:, :, E:2 * E], comb[:, :, :], combr[:, :, :].bitcast(f32), ALU.subtract).then_inc(comb_ready, 1)

            def combine(c, o, e, own):
                a = cols["moe_b2"][0] + e
                dve.wait_ge(down2_done, o * E + e + 1)
                dve.wait_ge(cb_ready, o * E + e + 1)
                dst = acc if e == 0 else scaled
                dve.scalar_tensor_tensor(out=dst[:, :], in0=bank[5][:, :], scalar=wp[:, a:a + 1], in1=cbs[:, :],
                                         op0=ALU.add, op1=ALU.mult).then_inc(y_used, 1)
                if e:
                    dve.wait_ge(y_used, o * E + e + 1)
                    dve.tensor_tensor(acc[:, :], acc[:, :], scaled[:, :], ALU.add).then_inc(acc_done, 1)
                else:
                    dve.wait_ge(y_used, o * E + e + 1)

            def iteration(c, own):
                new = has(c - 1, c)
                for u in range(NU2):
                    oe = expert_at(c, u)
                    if oe:
                        o, e = oe
                        for k in range(HB // 2, HB):
                            a = cols["moe_b1"][0] + HB * e + k
                            dve.wait_ge(up2_done, o * (E * HB) + HB * e + k + 1)
                            dve.tensor_scalar(hT[:, k, :], bank[1 + k][:, :], wp[:, a:a + 1], 0.0, ALU.add, ALU.max).then_inc(h2v_ready, 1)
                    if u == 2 and new:
                        dve.wait_ge(zhi_ready, c)
                        dve.tensor_tensor(zlo[:, :], zT[:, :], zhi[:, :].bitcast(f32), ALU.subtract).then_inc(zlo_ready, 1)
                        combine_weights(c, own)
                    if u == 3 and has(c - 2, c):
                        dve.wait_ge(final_done, c - 1)
                        if not isinstance(c, int) or c > 2:
                            dve.wait_ge(stored, 16 * (c - 2))
                        dve.tensor_tensor(outt[:, :, :], bank[6][:, :].rearrange("p (t d) -> p t d", t=CT), XU[:, tiles(c, 2), :],
                                          ALU.add).then_inc(out_ready, 1)
                    half, k = u // 4, u % 4
                    if has(c + half, c):
                        cc, b = c + half, 4 * (1 - half)
                        if k == 0:
                            mask(cc, b + 2)
                            mask(cc, b + 3)
                        if k >= 2:
                            square(cc, b + 2 * k - 4)
                            square(cc, b + 2 * k - 3)
                    if k in (1, 2) and has(c + 1, c):
                        mask(c + 1, 4 * half + k - 1)
                    if u == 0 and new:
                        chunk_norm(c, own)
                    if u == 1 and new:
                        choose(c, own)
                    if oe:
                        combine(c, *oe, own)

            iteration(0, own)
            iteration(1, own)
            iteration(2, own)
            k0 = own.k
            PER3 = 1 + CT + 6 + 15 + 1 + 1 + 2 * CT + 1 + 7 + 2
            with dve.Fori(3, NC - 1) as c:
                it = Steps(dve, dve_s, (c - 3) * PER3 + k0)
                iteration(c, it)
                assert it.k == PER3, it.k
            own.k = k0 + (NC - 4) * PER3
            for c in range(NC - 1, NC + 2):
                iteration(c, own)

        @block.tensor
        def _(pe):
            def split3(dst, whi, wlo, mhi, mlo, start, stop):
                pe.matmul(dst, whi, mhi, start=start, stop=False)
                pe.matmul(dst, whi, mlo, start=False, stop=False)
                return pe.matmul(dst, wlo, mhi, start=False, stop=stop)

            def main1(c, p):
                r = p % R1
                pe.wait_ge(lo_ready, c * NU1 + p + 1)
                if c is 0 and p % 2 == 0:
                    pe.wait_ge(x2lo_r, p // 2 + 1)
                    pe.wait_ge(x1lo_r, p // 2 + 1)
                for b in range(2):
                    if p == 0 and c is not 0:
                        pe.wait_ge(ax_evac, 2 * c - 1 + b)
                    for t in range(U1):
                        j = p * U1 + t
                        last = split3(bank[b][:, :], xhi[b][:, j, :], xlo[b][:, j, :],
                                      ahi[r][:, t * CW:(t + 1) * CW], alo[r][:, t * CW:(t + 1) * CW],
                                      p == 0 and t == 0, p == NU1 - 1 and t == U1 - 1)
                    if p == NU1 - 1 and b == 0:
                        last.then_inc(ax0_done, 1)
                last.then_inc(unit_done, 1)

            def post1(c, p):
                if p in (0, 2, 4):
                    i = p // 2
                    if i:
                        pe.wait_ge(m_ready, 6 * c - 6 + 2 * i)
                    for b in range(2):
                        last = pe.matmul(bank[2 + b][:, :], gnnw[b][i], ms[:, b, :], start=True, stop=True)
                    last.then_inc(lay_done, 1)
                if p == 6:
                    pe.wait_ge(m_ready, 6 * c)
                    pe.wait_ge(v_done, c)
                    for t in range(CT):
                        for b in range(2):
                            last = pe.matmul(bank[4][:, t * D:(t + 1) * D], ms[:, b, t * P:(t + 1) * P], mergew[b],
                                             start=b == 0, stop=b == 1)
                    last.then_inc(merge_done, 1)
                if p == 9:
                    pe.wait_ge(z1_ready, CT * c)
                    for t in range(CT):
                        last = pe.transpose(bank[5][:, t * P:(t + 1) * P], z[:, t, :], ident[:, :])
                    last.then_inc(zT_done, 1)
                if p == 11:
                    pe.wait_ge(zT_ready, c)
                    for k in range(HB):
                        a = cols["ffn_w1"][0] + k * P
                        pe.matmul(bank[(2, 3, 6, 7)[k]][:, :], wp[:, a:a + P], zT[:, :], start=True, stop=True).then_inc(up_done, 1)
                if p == 13:
                    pe.wait_ge(h_ready, HB * c)
                    for t in range(CT):
                        for k in range(HB):
                            a = cols["ffn_w2"][0] + k * D
                            pe.matmul(bank[5][:, t * D:(t + 1) * D], hT[:, k, t * P:(t + 1) * P], wp[:, a:a + D],
                                      start=k == 0, stop=k == HB - 1)
                    for t in range(CT):
                        last = pe.matmul(bank[4][:, t:t + 1], zT[:, t * P:(t + 1) * P], W("wr"), start=True, stop=True)
                    last.then_inc(down_done, 1)

            for p in range(NU1):
                main1(0, p)
            pe.wait_ge(wp_in, 16)
            pe.wait_ge(consts, 4 + CT)
            with pe.Fori(1, NC) as c:
                for p in range(NU1):
                    main1(c, p)
                    post1(c, p)
            for p in range(NU1):
                if p == 0:
                    pe.wait_ge(ax_evac, 2 * NC)
                post1(NC, p)

            for n in range(10):
                pe.wait_ge(cnt_ready, n + 1)
                if n == 4:
                    last = pe.matmul(bank[6][:, 0:1], ones[:, :], cnt[:, 0:1], start=True, stop=True)
                elif n < 9:
                    last = pe.matmul(bank[6][:, 0:15], ones[:, :], cnt[:, :], start=True, stop=True)
                else:
                    pe.matmul(bank[6][:, 64:64 + T], before[:, :], eqc[:, 0:T], start=True, stop=True)
                    last = pe.matmul(bank[6][:, 0:T + 1], ones[:, :], eqc[:, :], start=True, stop=True)
                last.then_inc(cnt_done, 1)
            with pe.Fori(0, NC // 2) as i:
                for b in range(2):
                    pe.wait_ge(z2_ready, i * (2 * CT) + CT * b + CT)
                    for t in range(CT):
                        last = pe.transpose(bank[5 + b][:, t * P:(t + 1) * P], (z, outt)[b][:, t, :], ident[:, :])
                    last.then_inc(z2T_done, 1)
                for b in range(2):
                    pe.wait_ge(z2T_ready, 2 * i + b + 1)
                    pe.wait_ge(msg_ready, 2 * i + b + 1)
                    src = (zT[:, :], ms[:, 0, :])[b]
                    for t in range(CT):
                        last = pe.matmul(bank[3 + b][:, t * D:(t + 1) * D], src[:, t * P:(t + 1) * P], W("gnnW"), start=True, stop=True)
                    last.then_inc(msg_done, 1)
            pe.wait_ge(msg_ready, NC + 2)

            def iteration(c):
                new = has(c - 1, c)
                for u in range(NU2):
                    oe = expert_at(c, u)
                    if oe:
                        o, e = oe
                        if e == 0:
                            pe.wait_ge(zlo_ready, c)
                            pe.wait_ge(cT_ready, c)
                            if c is 1:
                                pe.wait_ge(w1_ready, 5)
                                pe.wait_ge(moe2_in, 16)
                        for k in range(HB):
                            split3(bank[1 + k][:, :], w1hi[:, e, k * P:(k + 1) * P], w1lo[:, e, k * P:(k + 1) * P],
                                   zhi[:, :], zlo[:, :], True, True).then_inc(up2_done, 1)
                        if not (isinstance(o, int) and o == 0 and e == 0):
                            pe.wait_ge(cb_ready, o * E + e)
                        pe.matmul(bank[7][:, :], pick[:, e, :], cTs[:, :], start=True, stop=True).then_inc(cb_done, 1)
                    if u == 1 and new:
                        pe.wait_ge(z3_ready, CT * c)
                        for t in range(CT):
                            last = pe.transpose(bank[6][:, t * P:(t + 1) * P], z[:, t, :], ident[:, :])
                        last.then_inc(t2_done, 1)
                    if u == 3 and has(c - 2, c):
                        pe.wait_ge(acc_done, (E - 1) * (c - 1))
                        for t in range(CT):
                            last = pe.transpose(bank[6][:, t * P:(t + 1) * P], acc[:, t * P:(t + 1) * P], ident[:, :])
                        last.then_inc(final_done, 1)
                    if has(c, c):
                        pe.wait_ge(wt_ready, c * NU2 + u + 1)
                        if u == 0 and new:
                            pe.wait_ge(g_evac, c)
                        for t in range(U2):
                            last = pe.matmul(bank[0][:, :], VM[:, u * U2 + t, :], wt[u][:, t * CW:(t + 1) * CW],
                                             start=u == 0 and t == 0, stop=u == NU2 - 1 and t == U2 - 1)
                        last.then_inc(wt_used, 1)
                    if u == 0 and new:
                        pe.wait_ge(g_evac, c)
                        for t in range(CT):
                            last = pe.transpose(bank[6][:, t * P:(t + 1) * P], ms[:, 0, t * P:(t + 1) * P], ident[:, :])
                        last.then_inc(t1_done, 1)
                    if u == 1 and new:
                        pe.wait_ge(zT2_ready, c)
                        for t in range(CT):
                            last = pe.matmul(bank[6][:, t * E:(t + 1) * E], zT[:, t * P:(t + 1) * P], W("Wg"), start=True, stop=True)
                        last.then_inc(gate_done, 1)
                    if oe:
                        pe.wait_ge(h2a_ready, o * (E * HB // 2) + HB // 2 * (e + 1))
                        pe.wait_ge(h2v_ready, o * (E * HB // 2) + HB // 2 * (e + 1))
                        if not (isinstance(o, int) and o == 0 and e == 0):
                            pe.wait_ge(y_used, o * E + e)
                        for k in range(HB):
                            last = pe.matmul(bank[5][:, :], w2[:, e, k, :], hT[:, k, :], start=k == 0, stop=k == HB - 1)
                        last.then_inc(down2_done, 1)
                    if u == 2 and new:
                        pe.wait_ge(comb_ready, 2 * c)
                        for t in range(CT):
                            last = pe.transpose(bank[6][0:2 * E, t * P:(t + 1) * P], comb2[:, t, :], ident[:, :])
                        last.then_inc(cT_done, 1)

            iteration(0)
            iteration(1)
            with pe.Fori(2, NC - 1) as c:
                iteration(c)
            for c in range(NC - 1, NC + 2):
                iteration(c)


def kernel(**inputs):
    import numpy as np
    import concourse.bacc as bacc
    from concourse import mybir
    from concourse.bass_utils import run_bass_kernel_spmd as run

    g = {k: np.asarray(v) for k, v in inputs.items()}
    P, CW = 128, 512
    N = g["adj"].shape[0]
    adj_tiles = np.ascontiguousarray(
        g["adj"].T.reshape(N // (2 * P), 2, P, N // CW, CW).transpose(3, 0, 2, 1, 4)).reshape(-1, P, 2 * CW)

    cols, parts, at = {}, [], 0
    for name, a in (
            ("gnn0", g["L0_gnn_W1"].transpose(2, 0, 1).reshape(P, -1)),
            ("gnn1", g["L0_gnn_W2"].transpose(2, 0, 1).reshape(P, -1)),
            ("merge", g["L0_gnn_Wm"].T.reshape(2, P, P).transpose(1, 0, 2).reshape(P, -1)),
            ("gnnW", g["L1_gnn_W"]),
            ("ffn_w1", g["L0_ffn_w1"]),
            ("ffn_w2", g["L0_ffn_w2"].reshape(4, P, P).transpose(1, 0, 2).reshape(P, -1)),
            ("gnnb0", g["L0_gnn_b1"].T), ("gnnb1", g["L0_gnn_b2"].T),
            ("ffn_b1", g["L0_ffn_b1"].reshape(4, P).T),
            ("wr", g["L0_ffn_wr"]),
            ("Wg", g["L1_ffn_Wg"].T),
            ("moe_b1", g["L1_ffn_b1"].reshape(8 * 4, P).T),
            ("moe_b2", g["L1_ffn_b2"].T)):
        cols[name] = (at, at + a.shape[1])
        at += a.shape[1]
        parts.append(a)
    wpack = np.ascontiguousarray(np.concatenate(parts, axis=1))
    rows, parts, at = {}, [], 0
    for name, names in (("bm", ["L0_gnn_bm"]), ("ffn_b2", ["L0_ffn_b2"]), ("B", ["L1_gnn_B"]), ("bg", ["L1_ffn_bg"]),
                        ("br", ["L0_ffn_br"]), ("eps", ["L0_gnn_eps1", "L0_gnn_eps2"])):
        a = np.concatenate([g[n] for n in names])
        rows[name] = (at, at + a.size)
        at += a.size
        parts.append(a)
    rowpack = np.concatenate(parts)[None, :]
    w1 = np.ascontiguousarray(g["L1_ffn_W1"].transpose(2, 0, 1))
    w2 = np.ascontiguousarray(g["L1_ffn_W2"].reshape(8, P, 4, P).transpose(3, 0, 2, 1))

    nc = bacc.Bacc("TRN2", target_bir_lowering=False, num_devices=1)
    arrays, args = {}, []
    for name, a in (("adj_tiles", adj_tiles), ("x", g["x"]), ("x2", g["L0_gnn_x2"]), ("wpack", wpack), ("rowpack", rowpack),
                    ("moe_w1", w1), ("moe_w2", w2)):
        arrays[name + "_dram"] = np.ascontiguousarray(a)
        args.append(nc.dram_tensor(name + "_dram", a.shape, mybir.dt.float32, kind="ExternalInput").ap())
    args.append(nc.dram_tensor("out_dram", (N, P), mybir.dt.float32, kind="ExternalOutput").ap())
    build_program(nc, *args, cols, rows)
    return run(nc, [arrays], core_ids=[0]).results[0]["out_dram"]
```

```python
import concourse.bass as bass
from concourse import mybir
from contextlib import ExitStack


class Steps:

    def __init__(self, eng, sem, base):
        self.eng, self.sem, self.base, self.k = eng, sem, base, 0

    def do(self, ins):
        ins.then_inc(self.sem, 1)
        self.k += 1

    def wait(self):
        self.eng.wait_ge(self.sem, self.base + self.k)

    def link(self, ins):
        self.do(ins)
        self.wait()


def build_program(nc, adj_tiles, x_in, x2_in, wpack_in, rows_in, moe_w1_in, moe_w2_in, out, cols, first_cols, rows):
    f32, f32r, bf16 = mybir.dt.float32, mybir.dt.float32r, mybir.dt.bfloat16
    i32, u32 = mybir.dt.int32, mybir.dt.uint32
    ALU = mybir.AluOpType
    ACT = mybir.ActivationFunctionType
    AX = mybir.AxisListType.X
    ds = bass.ds

    N, D = x_in.shape
    P = 128
    T = N // P
    CW = 512
    NC = N // CW
    CT = CW // P
    U1 = 2
    NU1 = T // U1
    T0 = 12
    T2 = 8
    U2 = 4
    NU2 = T // U2
    E = moe_w1_in.shape[1]
    HB = 4
    KEEP = N // 2 - 1
    EPS = 1e-5
    A1, R1 = 8, 4
    M0 = 5
    S0 = 3
    LAG = 3
    TINY = 1e-18
    assert NU2 == E == 8 and NU1 == 16

    x_v = x_in.rearrange("(t p) d -> p t d", p=P)
    x2_v = x2_in.rearrange("(t p) d -> p t d", p=P)
    out_v = out.rearrange("(c t p) d -> c p t d", t=CT, p=P)

    ctx = ExitStack()
    with ctx:
        def sb(name, shape, dt=f32):
            return ctx.enter_context(nc.sbuf_tensor(name, shape, dt))

        def sem(name):
            return ctx.enter_context(nc.semaphore(name))

        wp = sb("wp", [P, wpack_in.shape[1] - first_cols])
        rw = sb("rw", [P, rows_in.shape[1]])
        ident = sb("ident", [P, P])
        ones = sb("ones", [P, P])
        ones16 = sb("ones16", [P, P], bf16)
        before = sb("before", [P, P], bf16)
        XU = sb("XU", [P, T, D])
        VM = sb("VM", [P, T, D])
        ms = sb("ms", [P, 2, CW])
        hT = sb("hT", [P, HB, CW])
        z = sb("z", [P, CT, D])
        zT = sb("zT", [P, CW])
        x3 = sb("x3", [P, CT, D])
        outt = sb("outt", [P, CT, D])
        nmr = sb("nmr", [P, T])
        rsx = sb("rsx", [P, T])
        bn6 = sb("bn6", [P, T, 6])
        bnx = sb("bnx", [P, 2 * T, 6])
        mv = sb("mv", [P, 2 * T, 2])
        rs_v = sb("rs_v", [P, 2 * T])
        rs_y = sb("rs_y", [P, 2 * T])
        rs_t = sb("rs_t", [P, 2 * T])
        scale12 = sb("scale12", [P, 2])
        cp = sb("cp", [P, 1])
        cb = sb("cb", [P, 3])
        rsum = sb("rsum", [P, CT])
        wtok = sb("wtok", [P, T])
        key = sb("key", [P, T], i32)
        keyt = sb("keyt", [P, T], i32)
        khi = sb("khi", [P, T])
        klo = sb("klo", [P, T])
        steps15 = sb("steps15", [P, 15])
        steps15i = sb("steps15i", [P, 15], i32)
        thr = sb("thr", [P, 15])
        cnt = sb("cnt", [P, 15], bf16)
        digit = sb("digit", [P, 1])
        Thi = sb("Thi", [P, 1])
        Tlo = sb("Tlo", [P, 1])
        kleft = sb("kleft", [P, 1])
        above = sb("above", [P, T])
        eqc = sb("eqc", [P, T + 1], bf16)
        tots = sb("tots", [P, T])
        rank = sb("rank", [P, T])
        sel = sb("sel", [P, T])
        gate = sb("gate", [P, CT, E])
        top8 = sb("top8", [P, CT, E])
        top8i = sb("top8i", [P, CT, E], u32)
        topf = sb("topf", [P, CT, E])
        iota8 = sb("iota8", [P, CT, E])
        iota8i = sb("iota8i", [P, E], i32)
        pd = sb("pd", [P, CT])
        pe2 = sb("pe2", [P, CT])
        ps1 = sb("ps1", [P, CT])
        prob = sb("prob", [P, 2, CT])
        hot = sb("hot", [P, CT, E])
        gap = sb("gap", [P, 1])
        comb = sb("comb", [P, CT, E])
        combr = sb("combr", [P, CT, E], f32r)
        comb2 = sb("comb2", [P, CT, 2 * E])

        first = ExitStack()
        wp1 = first.enter_context(nc.sbuf_tensor("wp1", [P, first_cols], f32))
        raw = [first.enter_context(nc.sbuf_tensor(f"raw{s}", [P, U1 * CW], f32)) for s in range(A1)]
        ahi = [first.enter_context(nc.sbuf_tensor(f"ahi{s}", [P, U1 * CW], f32r)) for s in range(R1)]
        alo = [first.enter_context(nc.sbuf_tensor(f"alo{s}", [P, U1 * CW], f32r)) for s in range(R1)]
        xhi = [first.enter_context(nc.sbuf_tensor(f"xhi{b}", [P, T, D], f32r)) for b in range(2)]
        xlo = [first.enter_context(nc.sbuf_tensor(f"xlo{b}", [P, T, D], f32r)) for b in range(2)]
        upw = [first.enter_context(nc.sbuf_tensor(f"upw{i}", [P, HB * P], f32r)) for i in range(2)]
        zp = [first.enter_context(nc.sbuf_tensor(f"zp{i}", [P, CW], f32r)) for i in range(2)]
        first.close()
        hhi = sb("hhi", [P, HB // 2, CW], f32r)
        hlo = sb("hlo", [P, HB // 2, CW], f32r)
        wt = [sb(f"wt{u}", [P, U2 * CW]) for u in range(NU2 - 1)]
        w1hi = sb("w1hi", [P, E, HB * P], f32r)
        w1lo = sb("w1lo", [P, E, HB * P], f32r)
        w2 = sb("w2", [P, E, HB // 2, D])
        w2hi = sb("w2hi", [P, E, HB // 2, D], f32r)
        w2lo = sb("w2lo", [P, E, HB // 2, D], f32r)
        pick = sb("pick", [2 * E, E, P], f32r)
        zhi = sb("zhi", [P, CW], f32r)
        zlo = sb("zlo", [P, CW], f32r)
        acc = sb("acc", [P, CW])
        cbs = sb("cbs", [P, CW])
        cTs = sb("cTs", [2 * E, CW], f32r)
        cmp = sb("cmp", [P, 15, T])
        sums = ExitStack()
        wt.append(sums.enter_context(nc.sbuf_tensor(f"wt{NU2 - 1}", [P, U2 * CW], f32)))
        sums.close()
        hhi2 = sb("hhi2", [P, HB // 2, CW], f32r)
        hlo2 = sb("hlo2", [P, HB // 2, CW], f32r)
        scaled = ms[:, 1, :]
        pickf = w2[0:2 * E, :, 0, :]

        bank = [ctx.enter_context(nc.psum_tensor(f"bank{i}", [P, 512], f32)) for i in range(8)]

        def W(name):
            a, b = cols[name]
            return wp[:, a:b]

        def R(name):
            a, b = rows[name]
            return rw[:, a:b]

        gnnw = [[wp1[:, cols[f"gnn{b}"][0] + D * i:cols[f"gnn{b}"][0] + D * (i + 1)] for i in range(3)] for b in range(2)]
        mergew = [wp1[:, cols["merge"][0] + D * b:cols["merge"][0] + D * (b + 1)] for b in range(2)]

        x_in_s, x2_in_s, wp_in, rw_in = sem("x_loaded"), sem("x2_loaded"), sem("wp_loaded"), sem("rows_loaded")
        adj_in = [sem(f"adj_in{s}") for s in range(A1)]
        w_in = [sem(f"wt_in{u}") for u in range(NU2)]
        moe1_in, moe2_in = sem("moe_w1_in"), sem("moe_w2_in")
        x_first_s, x2_first_s = sem("x_first_loaded"), sem("x2_first_loaded")
        nmr_ready, xu_ready, z2T_done = sem("nmr_ready"), sem("xu_ready"), sem("z2T_done")
        stored = sem("stored")
        consts = sem("consts")
        consts_v = sem("consts_v")
        x2hi_r, x2lo_r, x1n_r, x1hi_r, x1lo_r = sem("x2hi"), sem("x2lo"), sem("x1_norm"), sem("x1hi"), sem("x1lo")
        nmr1_ready = sem("nmr1_ready")
        hi_ready, lo_ready, unit_done = sem("hi_ready"), sem("lo_ready"), sem("unit_done")
        ax0_done, ax_evac, lay_done, m_ready = sem("ax0_done"), sem("ax_evac"), sem("lay_done"), sem("m_ready")
        merge_done, z1_ready, zT_done, zT_ready = sem("merge_done"), sem("z1_ready"), sem("zT_done"), sem("zT_ready")
        up_done, h_ready, down_done, v_done = sem("up_done"), sem("h_ready"), sem("down_done"), sem("v_done")
        upw_ready, zphi_ready, zplo_ready = sem("upw_ready"), sem("zphi_ready"), sem("zplo_ready")
        cnt_ready, cnt_done = sem("cnt_ready"), sem("cnt_done")
        z2_ready, z2T_ready, msg_done, msg_ready = sem("z2_ready"), sem("z2T_ready"), sem("msg_done"), sem("msg_ready")
        msk_ready, ln_done, rec_done, wt_ready, wt_used = sem("msk_ready"), sem("ln_done"), sem("rec_done"), sem("wt_ready"), sem("wt_used")
        sq_done, q_ready = sem("sq_done"), sem("q_ready")
        w1_ready = sem("w1_ready")
        hhi_ready, hlo_ready = sem("hhi_ready"), sem("hlo_ready")
        g_evac, t1_done, z3_ready, t2_done, zhi_ready, zlo_ready = sem("g_evac"), sem("t1_done"), sem("z3_ready"), sem("t2_done"), sem("zhi_ready"), sem("zlo_ready")
        gate_done, diff_ready, exp_ready, comb_ready, cT_done, cT_ready, zT2_ready = sem("gate_done"), sem("diff_ready"), sem("exp_ready"), sem("comb_ready"), sem("cT_done"), sem("cT_ready"), sem("zT2_ready")
        cb_done, cb_ready, final_done, out_ready = sem("cb_done"), sem("cb_ready"), sem("final_done"), sem("out_ready")
        up2_done, h2a_ready, h2v_ready, down2_done, y_used, acc_done = sem("up2_done"), sem("h2a_ready"), sem("h2v_ready"), sem("down2_done"), sem("y_used"), sem("acc_done")
        dve_s, pool_s = sem("dve_steps"), sem("pool_steps")

        block = ctx.enter_context(nc.Block())

        ALL1 = NC * NU1

        def has(chunk, c):
            return not isinstance(c, int) or 0 <= chunk < NC

        def expert_at(c, u):
            o, e = (c - 2, E - LAG + u) if u < LAG else (c - 1, u - LAG)
            return (o, e) if has(o, c) else None

        LAST = (NC - 1) * E - LAG

        def turn(o, e):
            return (o * E + e - LAST) % 2 if isinstance(o, int) and o * E + e >= LAST else 0

        def is_last(o, e):
            return isinstance(o, int) and o * E + e >= LAST

        def hidden(o, e, k):
            return wt[0][:, k * CW:(k + 1) * CW] if turn(o, e) else hT[:, k, :]

        def parts(o, e, k):
            hi, lo = (hhi2, hlo2) if turn(o, e) else (hhi, hlo)
            return hi[:, k, :], lo[:, k, :]

        def down_at(c, u):
            if not (isinstance(c, int) and c >= NC):
                return expert_at(c, u)
            if u == 0:
                return expert_at(c - 1, NU2 - 1) if c > NC else None
            return expert_at(c, u - 1)

        def early_at(c, u, moved):
            if isinstance(c, int) and c == 1 and u < LAG + 2:
                return (0, moved.index(u)) if u in moved else None
            return expert_at(c, u)

        @block.sync
        def _(sp):
            sp.dma_start(VM[:, 0:T2, :], x2_v[:, 0:T2, :]).then_inc(x2_first_s, 16)

            def load1(c, p, off):
                if not isinstance(c, int) or c * NU1 + p >= A1:
                    sp.wait_ge(lo_ready, c * NU1 + p - (A1 - 1))
                sp.dma_start(raw[p % A1][:, :], adj_tiles[off, :, :]).then_inc(adj_in[p % A1], 16)

            for p in range(NU1):
                load1(0, p, p)
                if p == 0:
                    sp.dma_start(XU[:, 0:T0, :], x_v[:, 0:T0, :]).then_inc(x_first_s, 16)
                if p == 3:
                    sp.dma_start(XU[:, T0:T, :], x_v[:, T0:T, :]).then_inc(x_in_s, 16)
                    sp.dma_start(VM[:, T2:T, :], x2_v[:, T2:T, :]).then_inc(x2_in_s, 16)
                if p == 5:
                    sp.dma_start(rw[:, :], rows_in[0, :].partition_broadcast(P)).then_inc(rw_in, 16)
                if p == 7:
                    sp.dma_start(wp1[:, :], wpack_in[:, 0:first_cols]).then_inc(wp_in, 16)
                    sp.dma_start(wp[:, :], wpack_in[:, first_cols:]).then_inc(wp_in, 16)
            with sp.Fori(1, NC) as c:
                for p in range(NU1):
                    off = sp.snap(c * NU1 + p)
                    sp.wait_ge(lo_ready, c * NU1 + p - (A1 - 1))
                    sp.dma_start(raw[p % A1][:, :].rearrange("p (a f) -> p a f", a=1),
                                 adj_tiles[ds(off, 1), :, :].rearrange("a p f -> p a f")).then_inc(adj_in[p % A1], 16)

            sp.wait_ge(unit_done, ALL1)

            def load2(cc, u):
                src = adj_tiles[ds(cc * NU1 + 2 * u, 2), :, :] if not isinstance(cc, int) else adj_tiles[cc * NU1 + 2 * u:cc * NU1 + 2 * u + 2, :, :]
                return sp.dma_start(wt[u][:, :].rearrange("p (a f) -> p a f", a=2), src.rearrange("a p f -> p a f")).then_inc(w_in[u], 16)

            for u in range(NU2):
                load2(0, u)
            sp.wait_ge(down_done, NC)
            sp.dma_start(hT[:, :, :], moe_w1_in[:, 0:E // 2, :]).then_inc(moe1_in, 16)
            sp.wait_ge(w1_ready, 1)
            sp.dma_start(w2[:, :, :, :], moe_w1_in[:, E // 2:E, :].rearrange("p e (k d) -> p (e k) d", d=D).rearrange(
                "p (e k) d -> p e k d", k=HB // 2)).then_inc(moe1_in, 16)

            def store(o, ro):
                sp.wait_ge(out_ready, o + 1)
                dst = out_v[o, :, :, :] if isinstance(o, int) else out_v[ds(ro, 1), :, :, :].rearrange("a p t d -> p (a t) d")
                sp.dma_start(dst, outt[:, :, :]).then_inc(stored, 16)

            def iteration(c):
                for u in range(NU2):
                    if not isinstance(c, int):
                        off = sp.snap(c * NU1 + NU1 + 2 * u)
                        sp.wait_ge(wt_used, c * NU2 + u + 1)
                        sp.dma_start(wt[u][:, :].rearrange("p (a f) -> p a f", a=2),
                                     adj_tiles[ds(off, 2), :, :].rearrange("a p f -> p a f")).then_inc(w_in[u], 16)
                    elif c + 1 < NC:
                        sp.wait_ge(wt_used, c * NU2 + u + 1)
                        load2(c + 1, u)
                    if u == 4 and has(c - 2, c):
                        store(c - 2, None if isinstance(c, int) else sp.snap(c - 2))

            iteration(0)
            iteration(1)
            with sp.Fori(2, NC - 1) as c:
                iteration(c)
            for c in range(NC - 1, NC + 2):
                iteration(c)
            sp.wait_ge(stored, 16 * NC)

        @block.gpsimd
        def _(pool):
            own = Steps(pool, pool_s, 0)
            own.do(pool.memset(ident[:, :], 0.0))
            own.do(pool.memset(cp[:, 0:1], 0.0))
            pool.memset(ones[:, :], 1.0).then_inc(consts, 1)
            own.do(pool.memset(before[:, :], 1.0))
            own.do(pool.memset(ones16[:, :], 1.0))
            own.do(pool.iota(steps15i[:, :], pattern=[[1, 15]], base=1, channel_multiplier=0))
            own.do(pool.iota(iota8i[:, :], pattern=[[1, E]], base=0, channel_multiplier=0))
            own.wait()
            pool.affine_select(out=ident[:, :], in_=ident[:, :], compare_op=ALU.not_equal, fill=1.0, base=0,
                               pattern=[[-1, P]], channel_multiplier=1).then_inc(consts, 1)
            pool.affine_select(out=before[:, :], in_=before[:, :], compare_op=ALU.is_ge, fill=0.0, base=-1,
                               pattern=[[1, P]], channel_multiplier=-1).then_inc(consts, 1)
            pool.tensor_copy(steps15[:, :], steps15i[:, :]).then_inc(consts, 1)
            for t in range(CT):
                pool.tensor_copy(iota8[:, t, :], iota8i[:, :]).then_inc(consts, 1)

            def x2_low(g):
                s = slice(g * CT, (g + 1) * CT)
                pool.wait_ge(x2hi_r, g + 1)
                pool.tensor_tensor(xlo[1][:, s, :], VM[:, s, :], xhi[1][:, s, :].bitcast(f32), ALU.subtract).then_inc(x2lo_r, 1)

            def x1_low(g):
                s = slice(g * CT, (g + 1) * CT)
                pool.wait_ge(x1n_r, CT * (g + 1))
                pool.wait_ge(x1hi_r, g + 1)
                pool.tensor_tensor(xlo[0][:, s, :], hT[:, g % 4, :].rearrange("p (t d) -> p t d", t=CT),
                                   xhi[0][:, s, :].bitcast(f32), ALU.subtract).then_inc(x1lo_r, 1)

            x2_low(0)
            x2_low(1)
            x1_low(0)
            x1_low(1)
            for g in range(2, NC):
                x2_low(g)
                x1_low(g)
            a = cols["ffn_w1"][0]
            half_zero = cp[:, 0:1].to_broadcast([P, CW])
            pool.wait_ge(wp_in, 32)
            pool.tensor_tensor(upw[0][:, :], wp1[:, a:a + HB * P], half_zero, ALU.add).then_inc(upw_ready, 1)
            pool.wait_ge(upw_ready, 1)
            pool.tensor_tensor(upw[1][:, :], wp1[:, a:a + HB * P], upw[0][:, :].bitcast(f32), ALU.subtract).then_inc(upw_ready, 1)
            with pool.Fori(1, NC) as c:
                pool.wait_ge(zT_ready, c)
                pool.tensor_tensor(zp[0][:, :], zT[:, :], half_zero, ALU.add).then_inc(zphi_ready, 1)
                pool.wait_ge(zphi_ready, c)
                pool.tensor_tensor(zp[1][:, :], zT[:, :], zp[0][:, :].bitcast(f32), ALU.subtract).then_inc(zplo_ready, 1)
            pool.wait_ge(unit_done, ALL1)
            own.link(pool.memset(pickf, 0.0))
            for first_k in (0, E):
                own.link(pool.affine_select(out=pickf, in_=pickf, compare_op=ALU.not_equal, fill=1.0,
                                            base=-first_k, pattern=[[-1, E], [0, P]], channel_multiplier=1))
            pool.tensor_copy(pick[:, :, :], pickf).then_inc(w1_ready, 1)
            pool.wait_ge(msg_ready, NC + 2)
            zero = cp[:, 0:1].to_broadcast([P, CW])

            def split_weights(src, hi, lo, ready):
                for i in range(HB):
                    w = slice(i * CW, (i + 1) * CW)
                    pool.tensor_tensor(hi[:, w], src[:, w], zero, ALU.add).then_inc(w1_ready, 1)
                    pool.wait_ge(w1_ready, ready + 2 * i + 1)
                    pool.tensor_tensor(lo[:, w], src[:, w], hi[:, w].bitcast(f32), ALU.subtract).then_inc(w1_ready, 1)

            in_hT, in_w2 = hT[:, :, :].rearrange("p k t -> p (k t)"), w2[:, :, :, :].rearrange("p e k d -> p (e k d)")
            pool.wait_ge(moe1_in, 32)
            for h in range(2):
                split_weights((in_hT, in_w2)[h], *(w[:, h * E // 2:(h + 1) * E // 2, :].rearrange("p e h -> p (e h)") for w in (w1hi, w1lo)),
                              1 + 2 * HB * h)
            pool.wait_ge(moe1_in, 48)
            split_weights(in_hT, *(w[:, :, :, :].rearrange("p e k d -> p (e k d)") for w in (w2hi, w2lo)), 1 + 4 * HB)

            def split_hidden(o, e):
                for k in range(HB // 2):
                    n = o * (E * HB // 2) + HB // 2 * e + k
                    pool.wait_ge(h2a_ready, n + 1)
                    pool.wait_ge(hhi_ready, n + 1)
                    hi, lo = parts(o, e, k)
                    pool.tensor_tensor(lo, hidden(o, e, k), hi.bitcast(f32), ALU.subtract).then_inc(hlo_ready, 1)

            for e in range(E):
                split_hidden(0, e)
            with pool.Fori(1, NC - 2) as o:
                for e in range(E):
                    split_hidden(o, e)
            for o in (NC - 2, NC - 1):
                for e in range(E):
                    split_hidden(o, e)

        @block.scalar
        def _(act):
            def x2_high(g):
                if g * CT in (0, T2):
                    act.wait_ge(x2_first_s if g == 0 else x2_in_s, 16)
                s = slice(g * CT, (g + 1) * CT)
                act.activation(xhi[1][:, s, :], VM[:, s, :], ACT.Copy).then_inc(x2hi_r, 1)

            def x1_high(g):
                if g * CT in (0, T0):
                    act.wait_ge(nmr1_ready, 1 if g == 0 else 2)
                if g >= 4:
                    act.wait_ge(x1lo_r, g - 3)
                for k in range(CT):
                    t = g * CT + k
                    act.activation(hT[:, g % 4, k * D:(k + 1) * D], XU[:, t, :], ACT.Identity, bias=nmr[:, t:t + 1],
                                   scale=rs_y[:, t:t + 1]).then_inc(x1n_r, 1)
                act.wait_ge(x1n_r, CT * (g + 1))
                act.activation(xhi[0][:, g * CT:(g + 1) * CT, :], hT[:, g % 4, :], ACT.Copy).then_inc(x1hi_r, 1)

            def hi(c, p):
                act.wait_ge(adj_in[p % A1], 16 * (2 * c + p // A1 + 1))
                if not isinstance(c, int) or c * NU1 + p >= R1:
                    act.wait_ge(unit_done, c * NU1 + p - (R1 - 1))
                act.activation(ahi[p % R1][:, :], raw[p % A1][:, :], ACT.Copy).then_inc(hi_ready, 1)

            def ln(cc, u):
                act.wait_ge(msk_ready, cc * NU2 + u + 1)
                act.activation(wt[u][:, :], wt[u][:, :], ACT.Ln, bias=cb[:, 0:1]).then_inc(ln_done, 1)

            def rec(cc, u):
                act.wait_ge(ln_done, cc * NU2 + u + 1)
                act.activation(wt[u][:, :], wt[u][:, :], ACT.Exp, scale=-1.0).then_inc(rec_done, 1)

            def sens(cc, u):
                first = isinstance(cc, int) and cc == 0
                if first and u < S0:
                    act.wait_ge(sq_done, u + 1)
                else:
                    act.wait_ge(q_ready, cc * NU2 - S0 + u + 1)
                act.activation(wt[u][:, :], wt[u][:, :], ACT.Exp, scale=-2.0,
                               bias=0.0 if first and u < S0 else cb[:, 1:2]).then_inc(wt_ready, 1)

            def first_pass(c, main, post):
                for p in range(NU1):
                    if main and p != 3:
                        hi(c, p)
                    if post and p == 2:
                        act.wait_ge(ax0_done, c)
                        act.activation(ms[:, 0, :], bank[0][:, :], ACT.Copy, scale=scale12[:, 0:1]).then_inc(ax_evac, 1)
                        act.wait_ge(unit_done, c * NU1)
                        act.activation(ms[:, 1, :], bank[1][:, :], ACT.Copy, scale=scale12[:, 1:2]).then_inc(ax_evac, 1)
                    if main and p == 3:
                        hi(c, p)
                    if post and p in (3, 5, 7):
                        i = (p - 3) // 2
                        for b in range(2):
                            act.wait_ge(lay_done, 6 * c - 6 + 2 * i + b + 1)
                            a = cols[f"gnnb{b}"][0] + i
                            act.activation(ms[:, b, :], bank[2 + b][:, :], ACT.Relu, bias=wp[:, a:a + 1]).then_inc(m_ready, 1)
                    if post and not main and p == 8:
                        ln(0, 0)
                    if post and p == 12:
                        act.wait_ge(zT_done, c)
                        act.activation(zT[:, :], bank[5][:, :], ACT.Copy).then_inc(zT_ready, 1)
                    if post and p == 14:
                        for k in range(HB):
                            a = cols["ffn_b1"][0] + k
                            act.wait_ge(up_done, HB * c - HB + k + 1)
                            act.activation(hT[:, k, :], bank[(2, 3, 6, 7)[k]][:, :], ACT.Gelu_apprx_tanh,
                                           bias=wp[:, a:a + 1]).then_inc(h_ready, 1)

            for g in range(2):
                x2_high(g)
                hi(0, 2 * g)
                hi(0, 2 * g + 1)
            x1_high(0)
            x1_high(1)
            for g in range(2, NC):
                x2_high(g)
                hi(0, 2 * g)
                hi(0, 2 * g + 1)
                x1_high(g)
            with act.Fori(1, NC) as c:
                first_pass(c, True, True)
            first_pass(NC, False, True)

            def square(u):
                act.wait_ge(rec_done, u + 1)
                act.activation(wt[u][:, :], wt[u][:, :], ACT.Square, bias=cb[:, 2:3]).then_inc(sq_done, 1)

            rec(0, 0)
            square(0)
            for u in range(1, NU2):
                ln(0, u)
            for u in range(1, NU2):
                rec(0, u)
            sens(0, 0)
            square(1)
            sens(0, 1)
            square(2)

            act.wait_ge(nmr_ready, 1)
            with act.Fori(0, NC // 2) as i:
                for b in range(2):
                    act.wait_ge(xu_ready, i * (2 * CT) + b * CT + CT)
                    for k in range(CT):
                        t = i * (2 * CT) + b * CT + k
                        act.activation((z, outt)[b][:, k:k + 1, :], XU[:, ds(t, 1), :], ACT.Identity, bias=nmr[:, ds(t, 1)],
                                       scale=rsx[:, ds(t, 1)]).then_inc(z2_ready, 1)
                for b in range(2):
                    act.wait_ge(z2T_done, 2 * i + b + 1)
                    act.activation((zT[:, :], ms[:, 0, :])[b], bank[5 + b][:, :], ACT.Copy).then_inc(z2T_ready, 1)
            for u in range(2, NU2):
                sens(0, u)

            def evacuate(c):
                act.wait_ge(wt_used, c * NU2)
                act.activation(ms[:, 0, :], bank[0][:, :], ACT.Copy).then_inc(g_evac, 1)

            def feature_norm(c):
                act.wait_ge(t2_done, c)
                act.activation(zT[:, :], bank[6][:, :], ACT.Copy).then_inc(zT2_ready, 1)

            def high_z(c):
                act.wait_ge(zT2_ready, c)
                act.activation(zhi[:, :], zT[:, :], ACT.Copy).then_inc(zhi_ready, 1)

            def exp_gap(c):
                act.wait_ge(diff_ready, c)
                act.activation(pe2[:, :], pd[:, :], ACT.Exp).then_inc(exp_ready, 1)

            def combine_by_expert(c):
                act.wait_ge(cT_done, c)
                act.activation(cTs[:, :], bank[6][0:2 * E, :], ACT.Copy).then_inc(cT_ready, 1)

            def iteration(c):
                new = has(c - 1, c)
                first, second, end = (isinstance(c, int) and c == n for n in (0, 1, NC))
                for u in range(NU2):
                    if u == 0 and new and not second:
                        evacuate(c)
                    if second and u == 0:
                        for m in (4, 5, 6):
                            ln(1, m)
                        combine_by_expert(c)
                    if (oe := early_at(c, u, (0, 2))):
                        o, e = oe
                        for k in range(HB // 2):
                            a = cols["moe_b1"][0] + HB * e + k
                            act.wait_ge(up2_done, o * (E * HB) + HB * e + k + 1)
                            act.activation(hidden(o, e, k), bank[1 + k][:, :], ACT.Relu, bias=wp[:, a:a + 1]).then_inc(h2a_ready, 1)
                            act.activation(parts(o, e, k)[0], bank[1 + k][:, :], ACT.Relu, bias=wp[:, a:a + 1]).then_inc(hhi_ready, 1)
                        if end and u == 1:
                            feature_norm(c)
                        if end and u == 2:
                            act.wait_ge(up2_done, (o + 1) * (E * HB))
                            high_z(c)
                        act.wait_ge(cb_done, o * E + e + 1)
                        if not (isinstance(o, int) and o == 0 and e == 0):
                            act.wait_ge(y_used, o * E + e)
                        act.activation(cbs[:, :], bank[7][:, :], ACT.Copy).then_inc(cb_ready, 1)
                    if end and u == 1:
                        exp_gap(c)
                    if u == 1 and new and not second and not end:
                        feature_norm(c)
                    if u == 2 and new and not second and not end:
                        high_z(c)
                        exp_gap(c)
                    half, k = u // 4, u % 4
                    if has(c + half, c) and not (isinstance(c, int) and c == 0 and half == 0):
                        cc, b = c + half, 4 * (1 - half)
                        for fn, j in (((ln, 0), (ln, 1), (ln, 2)), ((ln, 3), (rec, 0), (rec, 1)),
                                      ((rec, 2), (rec, 3), (sens, 0)), ((sens, 1), (sens, 2), (sens, 3)))[k]:
                            if not (second and fn is ln and b + j in (4, 5, 6)):
                                fn(cc, b + j)
                            if first and fn is rec and j == 1:
                                evacuate(1)
                                act.wait_ge(w1_ready, 1 + 4 * HB)
                                act.dma_start(hT[:, :, :], moe_w2_in[:, 0, :, :].rearrange("p (k f) h -> p k (f h)", k=HB)).then_inc(moe1_in, 16)
                                act.dma_start(w2[:, :, :, :].rearrange("p e k d -> p e (k d)"), moe_w2_in[:, 1, :, :]).then_inc(moe2_in, 16)
                            if first and fn is sens and j == 0:
                                feature_norm(1)
                                high_z(1)
                            if first and fn is sens and j == 2:
                                exp_gap(1)
                    if u == 2 and new and not second:
                        combine_by_expert(c)

            iteration(0)
            iteration(1)
            with act.Fori(2, NC - 1) as c:
                iteration(c)
            for c in range(NC - 1, NC + 2):
                iteration(c)

        @block.vector
        def _(dve):
            own = Steps(dve, dve_s, 0)

            def rsqrt(own, var, n, a=0):
                rsqrt_start(own, var, n, a)
                newton(own, n, 3, a)

            def rsqrt_start(own, var, n, a=0):
                v, y, t = rs_v[:, a:a + n], rs_y[:, a:a + n], rs_t[:, a:a + n]
                own.link(dve.tensor_scalar(v, var, EPS, None, ALU.add))
                own.link(dve.tensor_scalar(t.bitcast(i32), v.bitcast(i32), 1, None, ALU.logical_shift_right))
                own.link(dve.tensor_scalar(y.bitcast(i32), t.bitcast(i32), -1.0, 1597463007.0 - 2.0 ** 31, ALU.mult, ALU.add))

            def newton(own, n, times, a=0):
                v, y, t = rs_v[:, a:a + n], rs_y[:, a:a + n], rs_t[:, a:a + n]
                for _ in range(times):
                    own.link(dve.scalar_tensor_tensor(out=t, in0=y, scalar=0.5, in1=y, op0=ALU.mult, op1=ALU.mult))
                    own.link(dve.tensor_tensor(t, t, v, ALU.mult))
                    own.link(dve.scalar_tensor_tensor(out=y, in0=t, scalar=1.5, in1=y, op0=ALU.subtract, op1=ALU.mult))

            def moments(own, n, bn=bn6, a=0):
                bn, m, v = bn[:, a:a + n, :], mv[:, a:a + n, 0], mv[:, a:a + n, 1]
                own.do(dve.tensor_tensor(m, bn[:, :, 1], bn[:, :, 4], ALU.add))
                own.do(dve.tensor_tensor(rs_t[:, a:a + n], bn[:, :, 2], bn[:, :, 5], ALU.add))
                own.link(dve.tensor_tensor(rs_y[:, a:a + n], bn[:, :, 1], bn[:, :, 4], ALU.subtract))
                own.do(dve.tensor_scalar(m, m, 0.5, None, ALU.mult))
                own.link(dve.scalar_tensor_tensor(out=rs_y[:, a:a + n], in0=rs_y[:, a:a + n], scalar=0.25, in1=rs_y[:, a:a + n],
                                                  op0=ALU.mult, op1=ALU.mult))
                own.link(dve.scalar_tensor_tensor(out=v, in0=rs_t[:, a:a + n], scalar=1.0 / D, in1=rs_y[:, a:a + n],
                                                  op0=ALU.mult, op1=ALU.add))

            def stats(own, src, n):
                for k in range(n):
                    own.do(dve.bn_stats(bn6[:, k, :], src(k)))
                own.wait()
                moments(own, n)

            own.do(dve.memset(cb[:, 0:1], TINY))
            own.do(dve.memset(cb[:, 1:2], -2.0))
            own.do(dve.memset(cb[:, 2:3], -1.0))
            def lo(c, p):
                dve.wait_ge(hi_ready, c * NU1 + p + 1)
                dve.tensor_tensor(alo[p % R1][:, :], raw[p % A1][:, :], ahi[p % R1][:, :].bitcast(f32), ALU.subtract).then_inc(lo_ready, 1)

            def x_stats(a, n):
                for t in range(a, a + n):
                    own.do(dve.bn_stats(bn6[:, t, :], XU[:, t, :]))

            def x_norm(a, n):
                own.wait()
                moments(own, n, bn6, a)
                rsqrt(own, mv[:, a:a + n, 1], n, a)
                dve.scalar_tensor_tensor(out=nmr[:, a:a + n], in0=mv[:, a:a + n, 0], scalar=-1.0, in1=rs_y[:, a:a + n],
                                         op0=ALU.mult, op1=ALU.mult).then_inc(nmr1_ready, 1)

            def tiles(c, back):
                return slice((c - back) * CT, (c - back + 1) * CT) if isinstance(c, int) else ds((c - back) * CT, CT)

            def mask(cc, u):
                dve.wait_ge(w_in[u], 16 * (cc + 1))
                dve.scalar_tensor_tensor(out=wt[u][:, :], in0=wt[u][:, :], scalar=1.0, in1=wt[u][:, :],
                                         op0=ALU.is_lt, op1=ALU.mult).then_inc(msk_ready, 1)

            def square(cc, u):
                dve.wait_ge(rec_done, cc * NU2 + u + 1)
                dve.scalar_tensor_tensor(out=wt[u][:, :], in0=wt[u][:, :], scalar=2.0, in1=wt[u][:, :],
                                         op0=ALU.subtract, op1=ALU.mult).then_inc(q_ready, 1)

            def first_pass(c, main, post, own):
                for p in range(NU1):
                    if main:
                        lo(c, p)
                    if post and p == 10:
                        u = XU[:, tiles(c, 1), :]
                        own.wait()
                        dve.wait_ge(merge_done, c)
                        own.link(dve.tensor_tensor(x3[:, :, :], bank[4][:, :].rearrange("p (t d) -> p t d", t=CT), u, ALU.add))
                        stats(own, lambda k: x3[:, k, :], CT)
                        rsqrt(own, mv[:, 0:CT, 1], CT)
                        for k in range(CT):
                            dve.tensor_scalar(z[:, k, :], x3[:, k, :], mv[:, k, 0:1], rs_y[:, k:k + 1], ALU.subtract, ALU.mult).then_inc(z1_ready, 1)
                        dve.wait_ge(z1_ready, CT * c)
                        own.link(dve.tensor_tensor(u, x3[:, :, :], z[:, :, :], ALU.add))
                    if post and p == 12:
                        own.link(dve.tensor_tensor(x3[:, :, :], z[:, :, :], R("wr").unsqueeze(1).to_broadcast([P, CT, D]), ALU.mult))
                        own.link(dve.tensor_reduce(out=rsum[:, :], in_=x3[:, :, :], op=ALU.add, axis=AX))
                        own.link(dve.tensor_tensor(wtok[:, tiles(c, 1)], rsum[:, :], R("br").to_broadcast([P, CT]), ALU.add))
                    if post and p == 13:
                        stats_before(c, own)
                    if post and not main and p in (9, 15):
                        for u in (range(0, 1) if p == 9 else range(1, M0)):
                            mask(0, u)
                    if post and p == 15:
                        y = VM[:, tiles(c, 1), :]
                        wv = wtok[:, tiles(c, 1)]
                        dve.wait_ge(down_done, c)
                        own.link(dve.tensor_tensor(y, bank[5][:, :].rearrange("p (t d) -> p t d", t=CT),
                                                   R("ffn_b2").unsqueeze(1).to_broadcast([P, CT, D]), ALU.add))
                        dve.tensor_tensor(y, y, wv.unsqueeze(2).to_broadcast([P, CT, D]), ALU.mult).then_inc(v_done, 1)
                        if main:
                            stats_after(c, own)

            def stats_after(c, own):
                u = XU[:, tiles(c, 1), :]
                dve.wait_ge(v_done, c + 1)
                own.link(dve.tensor_tensor(x3[:, :, :], u, VM[:, tiles(c, 1), :], ALU.add))
                for k in range(CT):
                    own.do(dve.bn_stats(bnx[:, ds(c * CT - CT + k + T, 1), :], x3[:, k:k + 1, :]))

            def stats_before(c, own):
                for k in range(CT):
                    t = c * CT - CT + k
                    own.do(dve.bn_stats(bnx[:, ds(t, 1), :], XU[:, ds(t, 1), :]))

            PER1 = 1 + CT + 6 + 12 + 1 + 3 + 1 + 1 + 2 * CT
            lo(0, 0)
            dve.wait_ge(x_first_s, 16)
            x_stats(0, T0)
            lo(0, 1)
            lo(0, 2)
            x_norm(0, T0)
            lo(0, 3)
            dve.wait_ge(x_in_s, 16)
            x_stats(T0, T - T0)
            x_norm(T0, T - T0)
            lo(0, 4)
            lo(0, 5)
            dve.wait_ge(rw_in, 16)
            dve.tensor_scalar(scale12[:, :], R("eps"), 1.0, 1.0, ALU.add, ALU.add).then_inc(consts_v, 1)
            for p in range(6, NU1):
                lo(0, p)
            dve.wait_ge(x1hi_r, NC)
            dve.tensor_tensor(XU[:, :, :], XU[:, :, :], R("bm").unsqueeze(1).to_broadcast([P, T, D]), ALU.add).then_inc(v_done, 1)
            dve.wait_ge(v_done, 1)
            k0 = own.k
            with dve.Fori(1, NC) as c:
                it = Steps(dve, dve_s, (c - 1) * PER1 + k0)
                first_pass(c, True, True, it)
                assert it.k == PER1, it.k
            own.k = k0 + (NC - 1) * PER1

            first_pass(NC, False, True, own)

            dve.wait_ge(consts, 4 + CT)
            dve.wait_ge(v_done, NC + 1)
            own.link(dve.tensor_scalar(keyt[:, :], wtok[:, :].bitcast(i32), 31, -2147483648, ALU.arith_shift_right, ALU.bitwise_or))
            own.link(dve.tensor_tensor(key[:, :], wtok[:, :].bitcast(i32), keyt[:, :], ALU.bitwise_xor))
            own.link(dve.tensor_scalar(keyt[:, :], key[:, :], 16, None, ALU.logical_shift_right))
            own.link(dve.tensor_copy(khi[:, :], keyt[:, :]))
            own.link(dve.tensor_scalar(key[:, :], key[:, :], 65535, None, ALU.bitwise_and))
            own.link(dve.tensor_copy(klo[:, :], key[:, :]))
            own.do(dve.memset(Thi[:, :], 0.0))
            own.do(dve.memset(Tlo[:, :], 1.0))
            own.link(dve.memset(kleft[:, :], float(KEEP)))
            asked = [0]

            def total(dst, src):
                with nc.allow_low_precision(reason="whole numbers up to 32"):
                    return dve.tensor_reduce(out=dst, in_=src, op=ALU.add, axis=AX)

            def count(ins):
                ins.then_inc(cnt_ready, 1)
                asked[0] += 1
                if asked[0] <= NU2 - M0:
                    mask(0, M0 - 1 + asked[0])
                if asked[0] == 4:
                    stats_after(NC, own)
                    own.wait()
                if asked[0] == 5:
                    moments(own, 2 * T, bnx)
                if asked[0] == 6:
                    rsqrt_start(own, mv[:, :, 1], 2 * T)
                if 7 <= asked[0] <= 9:
                    newton(own, 2 * T, 1)
                if asked[0] == 10:
                    own.link(dve.scalar_tensor_tensor(out=rs_v[:, :], in0=mv[:, :, 0], scalar=-1.0, in1=rs_y[:, :],
                                                      op0=ALU.mult, op1=ALU.mult))
                dve.wait_ge(cnt_done, asked[0])

            def search(vals, t_ap):
                for shift in (12, 8, 4, 0):
                    own.link(dve.tensor_scalar(thr[:, :], steps15[:, :], float(1 << shift), t_ap, ALU.mult, ALU.add))
                    own.link(dve.tensor_tensor(cmp[:, :, :], vals.unsqueeze(1).to_broadcast([P, 15, T]),
                                               thr[:, :].unsqueeze(2).to_broadcast([P, 15, T]), ALU.is_ge))
                    count(total(cnt[:, :], cmp[:, :, :]))
                    own.link(dve.tensor_scalar(thr[:, :], bank[6][:, 0:15], kleft[:, :], None, ALU.is_ge))
                    own.link(dve.tensor_reduce(out=digit[:, :], in_=thr[:, :], op=ALU.add, axis=AX))
                    own.link(dve.scalar_tensor_tensor(out=t_ap, in0=digit[:, :], scalar=float(1 << shift), in1=t_ap,
                                                      op0=ALU.mult, op1=ALU.add))

            search(khi[:, :], Thi[:, :])
            own.link(dve.tensor_scalar(above[:, :], khi[:, :], Thi[:, :], None, ALU.is_gt))
            count(total(cnt[:, 0:1], above[:, :]))
            own.do(dve.tensor_scalar(kleft[:, :], bank[6][:, 0:1], -1.0, float(KEEP), ALU.mult, ALU.add))
            own.link(dve.tensor_scalar(klo[:, :], klo[:, :], 1.0, None, ALU.add))
            own.link(dve.scalar_tensor_tensor(out=klo[:, :], in0=khi[:, :], scalar=Thi[:, :], in1=klo[:, :],
                                              op0=ALU.is_equal, op1=ALU.mult))
            search(klo[:, :], Tlo[:, :])
            own.do(dve.scalar_tensor_tensor(out=above[:, :], in0=klo[:, :], scalar=Tlo[:, :], in1=above[:, :],
                                            op0=ALU.is_gt, op1=ALU.add))
            own.link(dve.tensor_scalar(eqc[:, 0:T], klo[:, :], Tlo[:, :], None, ALU.is_equal))
            count(total(eqc[:, T:T + 1], above[:, :]))
            own.do(dve.tensor_scalar(kleft[:, :], bank[6][:, T:T + 1], -1.0, float(KEEP), ALU.mult, ALU.add))
            own.link(dve.tensor_copy(rank[:, :], bank[6][:, 0:T]))
            own.link(dve.tensor_tensor_scan(tots[:, :], ones[:, 0:T], rank[:, :], 0.0, ALU.mult, ALU.add))
            own.link(dve.tensor_tensor(tots[:, :], tots[:, :], rank[:, :], ALU.subtract))
            own.link(dve.tensor_tensor(rank[:, :], bank[6][:, 64:64 + T], tots[:, :], ALU.add))
            own.link(dve.scalar_tensor_tensor(out=sel[:, :], in0=rank[:, :], scalar=kleft[:, :], in1=eqc[:, 0:T],
                                              op0=ALU.is_lt, op1=ALU.mult))
            own.link(dve.tensor_tensor(sel[:, :], sel[:, :], above[:, :], ALU.add))

            own.do(dve.tensor_tensor(rsx[:, :], rs_y[:, T:2 * T], sel[:, :], ALU.mult))
            own.do(dve.tensor_tensor(nmr[:, :], rs_v[:, T:2 * T], sel[:, :], ALU.mult))
            own.link(dve.tensor_scalar(rs_t[:, 0:T], sel[:, :], -1.0, 1.0, ALU.mult, ALU.add))
            own.do(dve.tensor_tensor(rs_y[:, 0:T], rs_y[:, 0:T], rs_t[:, 0:T], ALU.mult))
            own.link(dve.tensor_tensor(rs_v[:, 0:T], rs_v[:, 0:T], rs_t[:, 0:T], ALU.mult))
            own.link(dve.tensor_tensor(rsx[:, :], rsx[:, :], rs_y[:, 0:T], ALU.add))
            dve.tensor_tensor(nmr[:, :], nmr[:, :], rs_v[:, 0:T], ALU.add).then_inc(nmr_ready, 1)

            G = 2 * CT

            def select(i):
                for k in range(G):
                    t = i * G + k
                    dve.scalar_tensor_tensor(out=XU[:, ds(t, 1), :], in0=VM[:, ds(t, 1), :], scalar=sel[:, ds(t, 1)],
                                             in1=XU[:, ds(t, 1), :], op0=ALU.mult, op1=ALU.add).then_inc(xu_ready, 1)

            def messages(i):
                for b in range(2):
                    dve.wait_ge(msg_done, 2 * i + b + 1)
                    dve.tensor_tensor(VM[:, ds(i * G + b * CT, CT), :], bank[3 + b][:, :].rearrange("p (t d) -> p t d", t=CT),
                                      R("B").unsqueeze(1).to_broadcast([P, CT, D]), ALU.add).then_inc(msg_ready, 1)

            for b in range(2):
                dve.memset(gap[:, :], 0.0).then_inc(msg_ready, 1)
                dve.wait_ge(msg_ready, b + 1)
            select(0)
            with dve.Fori(0, NC // 2 - 1) as i:
                select(i + 1)
                messages(i)
            messages(NC // 2 - 1)
            for u in range(S0, NU2):
                square(0, u)

            def chunk_norm(c, own):
                dve.wait_ge(t1_done, c)
                own.link(dve.tensor_tensor(x3[:, :, :], bank[6][:, :].rearrange("p (t d) -> p t d", t=CT),
                                           XU[:, tiles(c, 1), :], ALU.add))
                stats(own, lambda k: x3[:, k, :], CT)
                rsqrt(own, mv[:, 0:CT, 1], CT)
                for k in range(CT):
                    dve.tensor_scalar(z[:, k, :], x3[:, k, :], mv[:, k, 0:1], rs_y[:, k:k + 1],
                                      ALU.subtract, ALU.mult).then_inc(z3_ready, 1)
                own.do(dve.tensor_copy(XU[:, tiles(c, 1), :], x3[:, :, :]))

            def choose(c, own):
                dve.wait_ge(gate_done, c)
                own.link(dve.tensor_tensor(gate[:, :, :], bank[6][:, 0:CT * E].rearrange("p (t e) -> p t e", t=CT),
                                           R("bg").unsqueeze(1).to_broadcast([P, CT, E]), ALU.add))
                dve.memset(gap[:, :], 0.0)
                for t in range(CT):
                    own.do(dve.max(top8[:, t, :], gate[:, t, :]))
                own.wait()
                dve.tensor_tensor(pd[:, :], top8[:, :, 1], top8[:, :, 0], ALU.subtract).then_inc(diff_ready, 1)
                for t in range(CT):
                    own.do(dve.max_index(top8i[:, t, :], top8[:, t, :], gate[:, t, :]))
                own.wait()
                own.link(dve.tensor_copy(topf[:, :, :], top8i[:, :, :]))

            def combine_weights(c, own):
                dve.wait_ge(exp_ready, c)
                own.link(dve.tensor_scalar(ps1[:, :], pe2[:, :], 1.0, None, ALU.add))
                own.link(dve.reciprocal(prob[:, 0, :], ps1[:, :]))
                own.link(dve.tensor_tensor(prob[:, 1, :], pe2[:, :], prob[:, 0, :], ALU.mult))
                own.do(dve.tensor_tensor(hot[:, :, :], iota8[:, :, :], topf[:, :, 0:1].to_broadcast([P, CT, E]), ALU.is_equal))
                own.link(dve.tensor_tensor(comb[:, :, :], iota8[:, :, :], topf[:, :, 1:2].to_broadcast([P, CT, E]), ALU.is_equal))
                own.do(dve.tensor_tensor(hot[:, :, :], hot[:, :, :], prob[:, 0, :].unsqueeze(2).to_broadcast([P, CT, E]), ALU.mult))
                own.link(dve.tensor_tensor(comb[:, :, :], comb[:, :, :], prob[:, 1, :].unsqueeze(2).to_broadcast([P, CT, E]), ALU.mult))
                own.link(dve.tensor_tensor(comb[:, :, :], comb[:, :, :], hot[:, :, :], ALU.add))
                own.link(dve.tensor_copy(combr[:, :, :], comb[:, :, :]))
                dve.tensor_copy(comb2[:, :, 0:E], combr[:, :, :].bitcast(f32)).then_inc(comb_ready, 1)
                dve.tensor_tensor(comb2[:, :, E:2 * E], comb[:, :, :], combr[:, :, :].bitcast(f32), ALU.subtract).then_inc(comb_ready, 1)

            def combine(c, o, e, own):
                a = cols["moe_b2"][0] + e
                dve.wait_ge(down2_done, o * E + e + 1)
                dve.wait_ge(cb_ready, o * E + e + 1)
                if is_last(o, e) and e > 1:
                    dve.wait_ge(acc_done, o * (E - 1) + e - 1)
                dst = acc[:, :] if e == 0 else scaled
                dve.scalar_tensor_tensor(out=dst, in0=bank[5][:, :], scalar=wp[:, a:a + 1], in1=cbs[:, :],
                                         op0=ALU.add, op1=ALU.mult).then_inc(y_used, 1)
                if e:
                    dve.wait_ge(y_used, o * E + e + 1)
                    dve.tensor_tensor(acc[:, :], acc[:, :], scaled, ALU.add).then_inc(acc_done, 1)
                else:
                    dve.wait_ge(y_used, o * E + e + 1)

            def low_z(c):
                dve.wait_ge(zhi_ready, c)
                dve.tensor_tensor(zlo[:, :], zT[:, :], zhi[:, :].bitcast(f32), ALU.subtract).then_inc(zlo_ready, 1)

            def iteration(c, own):
                new = has(c - 1, c)
                first, second, end = (isinstance(c, int) and c == n for n in (0, 1, NC))
                for u in range(NU2):
                    oe = early_at(c, u, (0, 3))
                    if oe:
                        o, e = oe
                        for k in range(HB // 2, HB):
                            a = cols["moe_b1"][0] + HB * e + k
                            dve.wait_ge(up2_done, o * (E * HB) + HB * e + k + 1)
                            dve.tensor_scalar(hidden(o, e, k), bank[1 + k][:, :], wp[:, a:a + 1], 0.0, ALU.add, ALU.max).then_inc(h2v_ready, 1)
                    last = isinstance(c, int) and c >= NC
                    if end and u == 2:
                        low_z(c)
                    if last and (oe := down_at(c, u)):
                        combine(c, *oe, own)
                    if u == 2 and new and not second and not end:
                        low_z(c)
                        combine_weights(c, own)
                    half, k = u // 4, u % 4
                    if first and u == 5:
                        mask(1, 4)
                        square(1, 0)
                        chunk_norm(1, own)
                    if first and u == 6:
                        square(1, 1)
                        square(1, 2)
                        choose(1, own)
                    if first and u == 7:
                        square(1, 3)
                        low_z(1)
                        combine_weights(1, own)
                        for m in (5, 6, 7):
                            mask(1, m)
                    if has(c + half, c) and not (first and u != 4):
                        cc, b = c + half, 4 * (1 - half)
                        if k == 0 and not (second and u == 0):
                            mask(cc, b + 2)
                            mask(cc, b + 3)
                        if k >= 2:
                            square(cc, b + 2 * k - 4)
                            square(cc, b + 2 * k - 3)
                    if k in (1, 2) and has(c + 1, c) and not (first and half):
                        mask(c + 1, 4 * half + k - 1)
                    if u == 0 and new and not second:
                        chunk_norm(c, own)
                    if u == 1 and new and not second:
                        choose(c, own)
                        if end:
                            combine_weights(c, own)
                    if u == 3 and has(c - 2, c):
                        dve.wait_ge(final_done, c - 1)
                        if not isinstance(c, int) or c > 2:
                            dve.wait_ge(stored, 16 * (c - 2))
                        dve.tensor_tensor(outt[:, :, :], bank[6][:, :].rearrange("p (t d) -> p t d", t=CT), XU[:, tiles(c, 2), :],
                                          ALU.add).then_inc(out_ready, 1)
                    if not last and (oe := early_at(c, u, (1, 4))):
                        combine(c, *oe, own)

            iteration(0, own)
            iteration(1, own)
            iteration(2, own)
            k0 = own.k
            PER3 = 1 + CT + 6 + 12 + 1 + 1 + 2 * CT + 1 + 7 + 2
            with dve.Fori(3, NC - 1) as c:
                it = Steps(dve, dve_s, (c - 3) * PER3 + k0)
                iteration(c, it)
                assert it.k == PER3, it.k
            own.k = k0 + (NC - 4) * PER3
            for c in range(NC - 1, NC + 2):
                iteration(c, own)

        @block.tensor
        def _(pe):
            def split3(dst, whi, wlo, mhi, mlo, start, stop):
                pe.matmul(dst, whi, mhi, start=start, stop=False)
                pe.matmul(dst, whi, mlo, start=False, stop=False)
                return pe.matmul(dst, wlo, mhi, start=False, stop=stop)

            def branch1(c, p, b):
                r = p % R1
                if isinstance(c, int) and c == 0:
                    pe.wait_ge((x1lo_r, x2lo_r)[b], p // 2 + 1)
                if p == 0 and not (isinstance(c, int) and c == 0):
                    pe.wait_ge(ax_evac, 2 * c - 1 + b)
                for t in range(U1):
                    j = p * U1 + t
                    last = split3(bank[b][:, :], xhi[b][:, j, :], xlo[b][:, j, :],
                                  ahi[r][:, t * CW:(t + 1) * CW], alo[r][:, t * CW:(t + 1) * CW],
                                  p == 0 and t == 0, p == NU1 - 1 and t == U1 - 1)
                if p == NU1 - 1 and b == 0:
                    last.then_inc(ax0_done, 1)
                return last

            def main1(c, p):
                pe.wait_ge(lo_ready, c * NU1 + p + 1)
                branch1(c, p, 0)
                branch1(c, p, 1).then_inc(unit_done, 1)

            def post1(c, p):
                if p in (0, 2, 4):
                    i = p // 2
                    for b in range(2):
                        if i:
                            pe.wait_ge(m_ready, 6 * c - 6 + 2 * i - 1 + b)
                        elif not (isinstance(c, int) and c == 0):
                            pe.wait_ge(ax_evac, 2 * c - 1 + b)
                        pe.matmul(bank[2 + b][:, :], gnnw[b][i], ms[:, b, :], start=True, stop=True).then_inc(lay_done, 1)
                if p == 6:
                    pe.wait_ge(m_ready, 6 * c)
                    pe.wait_ge(v_done, c)
                    for t in range(CT):
                        for b in range(2):
                            last = pe.matmul(bank[4][:, t * D:(t + 1) * D], ms[:, b, t * P:(t + 1) * P], mergew[b],
                                             start=b == 0, stop=b == 1)
                    last.then_inc(merge_done, 1)
                if p == 9:
                    pe.wait_ge(z1_ready, CT * c)
                    for t in range(CT):
                        last = pe.transpose(bank[5][:, t * P:(t + 1) * P], z[:, t, :], ident[:, :])
                    last.then_inc(zT_done, 1)
                if p == 11:
                    pe.wait_ge(zT_ready if isinstance(c, int) else zplo_ready, c)
                    for k in range(HB):
                        a = cols["ffn_w1"][0] + k * P
                        if not isinstance(c, int):
                            w = slice(k * P, (k + 1) * P)
                            split3(bank[(2, 3, 6, 7)[k]][:, :], upw[0][:, w], upw[1][:, w], zp[0][:, :], zp[1][:, :],
                                   True, True).then_inc(up_done, 1)
                            continue
                        pe.matmul(bank[(2, 3, 6, 7)[k]][:, :], wp1[:, a:a + P], zT[:, :], start=True, stop=True).then_inc(up_done, 1)
                if p == 12:
                    pe.wait_ge(h_ready, HB * c)
                    for t in range(CT):
                        for k in range(HB):
                            a = cols["ffn_w2"][0] + k * D
                            last = pe.matmul(bank[5][:, t * D:(t + 1) * D], hT[:, k, t * P:(t + 1) * P], wp1[:, a:a + D],
                                      start=k == 0, stop=k == HB - 1)
                    last.then_inc(down_done, 1)

            for units in (range(0, R1), range(R1, T0 // 2)):
                for p in units:
                    pe.wait_ge(lo_ready, p + 1)
                    branch1(0, p, 1)
                for p in units:
                    branch1(0, p, 0).then_inc(unit_done, 1)
            for p in range(T0 // 2, NU1):
                main1(0, p)
            pe.wait_ge(wp_in, 32)
            pe.wait_ge(upw_ready, 2)
            pe.wait_ge(consts, 4 + CT)
            with pe.Fori(1, NC) as c:
                for p in range(NU1):
                    main1(c, p)
                    post1(c, p)
            for p in range(NU1):
                post1(NC, p)

            for n in range(10):
                pe.wait_ge(cnt_ready, n + 1)
                if n == 4:
                    last = pe.matmul(bank[6][:, 0:1], ones16[:, :], cnt[:, 0:1], start=True, stop=True)
                elif n < 9:
                    last = pe.matmul(bank[6][:, 0:15], ones16[:, :], cnt[:, :], start=True, stop=True)
                else:
                    pe.matmul(bank[6][:, 64:64 + T], before[:, :], eqc[:, 0:T], start=True, stop=True)
                    last = pe.matmul(bank[6][:, 0:T + 1], ones16[:, :], eqc[:, :], start=True, stop=True)
                last.then_inc(cnt_done, 1)
            with pe.Fori(0, NC // 2) as i:
                for b in range(2):
                    pe.wait_ge(z2_ready, i * (2 * CT) + CT * b + CT)
                    for t in range(CT):
                        last = pe.transpose(bank[5 + b][:, t * P:(t + 1) * P], (z, outt)[b][:, t, :], ident[:, :])
                    last.then_inc(z2T_done, 1)
                for b in range(2):
                    pe.wait_ge(z2T_ready, 2 * i + b + 1)
                    pe.wait_ge(msg_ready, 2 * i + b + 1)
                    src = (zT[:, :], ms[:, 0, :])[b]
                    for t in range(CT):
                        last = pe.matmul(bank[3 + b][:, t * D:(t + 1) * D], src[:, t * P:(t + 1) * P], W("gnnW"), start=True, stop=True)
                    last.then_inc(msg_done, 1)
            pe.wait_ge(msg_ready, NC + 2)

            def turn_sum(c):
                pe.wait_ge(g_evac, c)
                for t in range(CT):
                    last = pe.transpose(bank[6][:, t * P:(t + 1) * P], ms[:, 0, t * P:(t + 1) * P], ident[:, :])
                last.then_inc(t1_done, 1)

            def turn_norm(c):
                pe.wait_ge(z3_ready, CT * c)
                for t in range(CT):
                    last = pe.transpose(bank[6][:, t * P:(t + 1) * P], z[:, t, :], ident[:, :])
                last.then_inc(t2_done, 1)

            def gate_scores(c):
                pe.wait_ge(zT2_ready, c)
                for t in range(CT):
                    last = pe.matmul(bank[6][:, t * E:(t + 1) * E], zT[:, t * P:(t + 1) * P], W("Wg"), start=True, stop=True)
                last.then_inc(gate_done, 1)

            def turn_combine(c):
                pe.wait_ge(comb_ready, 2 * c)
                for t in range(CT):
                    last = pe.transpose(bank[6][0:2 * E, t * P:(t + 1) * P], comb2[:, t, :], ident[:, :])
                last.then_inc(cT_done, 1)

            def down(o, e):
                if not (isinstance(o, int) and o == 0 and e == 0):
                    pe.wait_ge(y_used, o * E + e)
                for k in range(HB // 2, HB):
                    pe.wait_ge(h2v_ready, o * (E * HB // 2) + HB // 2 * e + k - 1)
                    pe.matmul(bank[5][:, :], w2[:, e, k - HB // 2, :], hidden(o, e, k), start=k == HB // 2, stop=False)
                for k in range(HB // 2):
                    pe.wait_ge(hlo_ready, o * (E * HB // 2) + HB // 2 * e + k + 1)
                    last = split3(bank[5][:, :], w2hi[:, e, k, :], w2lo[:, e, k, :], *parts(o, e, k), False, k == HB // 2 - 1)
                last.then_inc(down2_done, 1)

            def iteration(c):
                new = has(c - 1, c)
                second = isinstance(c, int) and c == 1
                for u in range(NU2):
                    oe = expert_at(c, u)
                    if oe:
                        o, e = oe
                        if e == 0:
                            pe.wait_ge(zlo_ready, c)
                            if second:
                                pe.wait_ge(w1_ready, 1 + 6 * HB)
                                pe.wait_ge(moe2_in, 16)
                        for k in range(HB):
                            if is_last(o, e):
                                pe.wait_ge((hhi_ready, h2v_ready)[k // 2], o * (E * HB // 2) + HB // 2 * (e - 1) + k % 2 + 1)
                            split3(bank[1 + k][:, :], w1hi[:, e, k * P:(k + 1) * P], w1lo[:, e, k * P:(k + 1) * P],
                                   zhi[:, :], zlo[:, :], True, True).then_inc(up2_done, 1)
                        if not (isinstance(o, int) and o == 0 and e == 0):
                            pe.wait_ge(cb_ready, o * E + e)
                        if e == 0:
                            pe.wait_ge(cT_ready, c)
                        pe.matmul(bank[7][:, :], pick[:, e, :], cTs[:, :], start=True, stop=True).then_inc(cb_done, 1)
                    after_sums = isinstance(c, int) and c >= NC
                    if after_sums and u == 2 and new:
                        turn_combine(c)
                    if after_sums and (late := down_at(c, u)):
                        down(*late)
                    if u == 1 and new and not second:
                        turn_norm(c)
                    if second and u == 0:
                        turn_sum(c)
                        turn_norm(c)
                        gate_scores(c)
                    if has(c, c):
                        pe.wait_ge(wt_ready, c * NU2 + u + 1)
                        if u == 0 and new:
                            pe.wait_ge(g_evac, c)
                        for t in range(U2):
                            last = pe.matmul(bank[0][:, :], VM[:, u * U2 + t, :], wt[u][:, t * CW:(t + 1) * CW],
                                             start=u == 0 and t == 0, stop=u == NU2 - 1 and t == U2 - 1)
                        last.then_inc(wt_used, 1)
                    if u == 3 and has(c - 2, c):
                        pe.wait_ge(acc_done, (E - 1) * (c - 1))
                        for t in range(CT):
                            last = pe.transpose(bank[6][:, t * P:(t + 1) * P], acc[:, t * P:(t + 1) * P], ident[:, :])
                        last.then_inc(final_done, 1)
                    if u == 0 and new and not second:
                        turn_sum(c)
                    if u == 1 and new and not second:
                        gate_scores(c)
                    if not after_sums and oe:
                        down(*oe)
                    if u == 2 and new and not after_sums:
                        turn_combine(c)

            iteration(0)
            iteration(1)
            with pe.Fori(2, NC - 1) as c:
                iteration(c)
            for c in range(NC - 1, NC + 2):
                iteration(c)


def kernel(**inputs):
    import numpy as np
    import concourse.bacc as bacc
    from concourse import mybir
    from concourse.bass_utils import run_bass_kernel_spmd as run

    g = {k: np.asarray(v) for k, v in inputs.items()}
    P, CW = 128, 512
    N = g["adj"].shape[0]
    adj_tiles = np.ascontiguousarray(
        g["adj"].T.reshape(N // (2 * P), 2, P, N // CW, CW).transpose(3, 0, 2, 1, 4)).reshape(-1, P, 2 * CW)

    cols, parts, at = {}, [], 0
    for name, a in (
            ("gnn0", g["L0_gnn_W1"].transpose(2, 0, 1).reshape(P, -1)),
            ("gnn1", g["L0_gnn_W2"].transpose(2, 0, 1).reshape(P, -1)),
            ("merge", g["L0_gnn_Wm"].T.reshape(2, P, P).transpose(1, 0, 2).reshape(P, -1)),
            ("ffn_w1", g["L0_ffn_w1"]),
            ("ffn_w2", g["L0_ffn_w2"].reshape(4, P, P).transpose(1, 0, 2).reshape(P, -1)),
            ("gnnW", g["L1_gnn_W"]),
            ("gnnb0", g["L0_gnn_b1"].T), ("gnnb1", g["L0_gnn_b2"].T),
            ("ffn_b1", g["L0_ffn_b1"].reshape(4, P).T),
            ("Wg", g["L1_ffn_Wg"].T),
            ("moe_b1", g["L1_ffn_b1"].reshape(8 * 4, P).T),
            ("moe_b2", g["L1_ffn_b2"].T)):
        if name == "gnnW":
            first_cols, at = at, 0
        cols[name] = (at, at + a.shape[1])
        at += a.shape[1]
        parts.append(a)
    wpack = np.ascontiguousarray(np.concatenate(parts, axis=1))
    rows, parts, at = {}, [], 0
    for name, names in (("bm", ["L0_gnn_bm"]), ("ffn_b2", ["L0_ffn_b2"]), ("B", ["L1_gnn_B"]), ("bg", ["L1_ffn_bg"]),
                        ("br", ["L0_ffn_br"]), ("wr", ["L0_ffn_wr"]), ("eps", ["L0_gnn_eps1", "L0_gnn_eps2"])):
        a = np.concatenate([g[n].reshape(-1) for n in names])
        rows[name] = (at, at + a.size)
        at += a.size
        parts.append(a)
    rowpack = np.concatenate(parts)[None, :]
    w1 = np.ascontiguousarray(g["L1_ffn_W1"].transpose(2, 0, 1))
    w2 = np.ascontiguousarray(g["L1_ffn_W2"].reshape(8, P, 2, 2, P).transpose(4, 2, 0, 3, 1)).reshape(P, 2, 8, -1)

    nc = bacc.Bacc("TRN2", target_bir_lowering=False, num_devices=1)
    arrays, args = {}, []
    for name, a in (("adj_tiles", adj_tiles), ("x", g["x"]), ("x2", g["L0_gnn_x2"]), ("wpack", wpack), ("rowpack", rowpack),
                    ("moe_w1", w1), ("moe_w2", w2)):
        arrays[name + "_dram"] = np.ascontiguousarray(a)
        args.append(nc.dram_tensor(name + "_dram", a.shape, mybir.dt.float32, kind="ExternalInput").ap())
    args.append(nc.dram_tensor("out_dram", (N, P), mybir.dt.float32, kind="ExternalOutput").ap())
    build_program(nc, *args, cols, first_cols, rows)
    return run(nc, [arrays], core_ids=[0]).results[0]["out_dram"]
```
